# Optimizing a Trainium2 kernel written in Bass

```python
import numpy as np
import jax
import jax.numpy as jnp

def _softmax(x, axis=-1):
    return jax.nn.softmax(x, axis=axis)

def _gelu(x):
    return jax.nn.gelu(x, approximate=True)

def _silu(x):
    return jax.nn.silu(x)

def _sigmoid(x):
    return jax.nn.sigmoid(x)

def _layernorm(x, axis=-1, eps=1e-05):
    m = jnp.mean(x, axis=axis, keepdims=True)
    v = jnp.var(x, axis=axis, keepdims=True)
    return (x - m) / jnp.sqrt(v + eps)

def _scatter_add(tgt, idx, src, axis=0):
    return tgt.at[idx].add(src)

def _segment_sum(src, seg, n):
    return jax.ops.segment_sum(src, seg, n)
kernel_name = 'mk_decoder_preln_d1_seqx_r4_faabf3'

def setup_inputs(seed: int=0):
    np.random.seed(seed)
    _w = jnp.asarray

    def _rec_inputs():
        import jax
        import jax.numpy as jnp
        _rk = jax.random.key(seed)
        x = 7.22e-05 + 1 * jax.random.normal(jax.random.fold_in(_rk, 1), (32, 128, 512), jnp.float32)
        _lenS = 128 - jax.random.randint(jax.random.fold_in(_rk, 7), (32,), 0, max(1, 128 // 4) + 1, jnp.int32)
        _lenS2 = 128 - jax.random.randint(jax.random.fold_in(_rk, 8), (32,), 0, max(1, 128 // 4) + 1, jnp.int32)
        _ctx_512P = jax.random.normal(jax.random.fold_in(_rk, 11), (32, 16, 128), jnp.float32)
        _ctx_512c = jax.random.dirichlet(jax.random.fold_in(_rk, 511), 0.3 * jnp.ones((16,), jnp.float32), (32, 128))
        _ctx_512t = jnp.einsum('bsk,bkd->bsd', _ctx_512c, _ctx_512P)
        _ctx_512t = _ctx_512t * jax.lax.rsqrt(jnp.mean(jnp.square(_ctx_512t)) + 1e-12) * 0.953939
        ctx_512 = -0.000514642 + 1.00011 * (_ctx_512t + 0.3 * jax.random.normal(jax.random.fold_in(_rk, 611), (32, 128, 128), jnp.float32))
        return (x, ctx_512)
    x, ctx_512 = _rec_inputs()

    def _L0_attn_setup():
        import jax, jax.numpy as jnp
        import numpy as np
        HID = 512
        H = 16
        D = HID // H
        THETA = 10000.0

        def _rope(q, k):
            T = q.shape[1]
            half = D // 2
            inv_freq = 1.0 / THETA ** (jnp.arange(half, dtype=jnp.float32) / half)
            ang = jnp.arange(T, dtype=jnp.float32)[:, None] * inv_freq[None, :]
            cos = jnp.cos(ang)[None, :, None, :]
            sin = jnp.sin(ang)[None, :, None, :]

            def rot(x):
                x1, x2 = (x[..., :half], x[..., half:])
                return jnp.concatenate([x1 * cos - x2 * sin, x2 * cos + x1 * sin], axis=-1)
            return (rot(q), rot(k))
        key = jax.random.key(seed)
        ks = jax.random.split(key, 7)
        B, T = (1, 512)
        s = 1.0 / np.sqrt(HID)
        return {'hidden_states': jax.random.normal(ks[0], (B, T, HID), dtype=jnp.float32), 'Wq': jax.random.normal(ks[1], (HID, HID), dtype=jnp.float32) * s, 'Wk': jax.random.normal(ks[2], (HID, HID), dtype=jnp.float32) * s, 'Wv': jax.random.normal(ks[3], (HID, HID), dtype=jnp.float32) * s, 'Wb': jax.random.normal(ks[4], (HID, H), dtype=jnp.float32) * s, 'bb': jnp.zeros((H,), dtype=jnp.float32), 'Wo': jax.random.normal(ks[5], (HID, HID), dtype=jnp.float32) * s}
    _L0_attn_all = _L0_attn_setup()
    _L0_attn_in = {k: v for k, v in _L0_attn_all.items() if k in ('Wq', 'Wk', 'Wv', 'Wb', 'bb', 'Wo')}
    del _L0_attn_all

    def _L0_xattn_setup():
        import jax, jax.numpy as jnp
        import numpy as np
        N_HEADS = 16
        N_KV_HEADS = 4
        ROPE_THETA = 10000.0
        EPS = 1e-05

        def _rms_norm(x, w):
            var = jnp.mean(x * x, axis=-1, keepdims=True)
            return x * jax.lax.rsqrt(var + EPS) * w

        def _rope_sin_cos(T, head_dim, dtype):
            inv_freq = 1.0 / ROPE_THETA ** (jnp.arange(0, head_dim, 2, dtype=jnp.float32) / head_dim)
            t = jnp.arange(T, dtype=jnp.float32)
            freqs = jnp.outer(t, inv_freq)
            emb = jnp.concatenate([freqs, freqs], -1)
            return (jnp.sin(emb).astype(dtype)[None, None], jnp.cos(emb).astype(dtype)[None, None])

        def _rotate_half(x):
            h = x.shape[-1] // 2
            x1, x2 = (x[..., :h], x[..., h:])
            return jnp.concatenate([-x2, x1], axis=-1)
        key = jax.random.key(seed)
        ks = jax.random.split(key, 6)
        B, T, C = (2, 512, 512)
        Ckv = C // N_HEADS * N_KV_HEADS
        return {'q': jax.random.normal(ks[0], (B, T, C), jnp.float32), 'k': jax.random.normal(ks[1], (B, T, Ckv), jnp.float32), 'v': jax.random.normal(ks[2], (B, T, Ckv), jnp.float32), 'q_norm_w': jnp.ones((C,), jnp.float32), 'k_norm_w': jnp.ones((Ckv,), jnp.float32), 'w_out': jax.random.normal(ks[3], (C, C), jnp.float32) * C ** (-0.5)}
    _L0_xattn_all = _L0_xattn_setup()
    _L0_xattn_in = {k: v for k, v in _L0_xattn_all.items() if k in ('q_norm_w', 'k_norm_w', 'w_out')}
    del _L0_xattn_all

    def _L0_ffn_setup():
        import jax, jax.numpy as jnp
        import numpy as np
        D = 512
        E = 8
        R = 16
        K = 2
        INIT_BONUS = 3.0
        ANNEAL_STEPS = 1250
        CURRENT_STEP = 1
        key = jax.random.key(seed)
        ks = jax.random.split(key, 7)
        s_in = 1.0 / np.sqrt(D)
        s_r = 1.0 / np.sqrt(R)
        return {'x': jax.random.normal(ks[0], (2, 1024, D), dtype=jnp.float32), 'Wr': jax.random.normal(ks[1], (D, E), dtype=jnp.float32) * s_in, 'br': jax.random.normal(ks[2], (E,), dtype=jnp.float32) * 0.01, 'Wd': jax.random.normal(ks[3], (E, D, R), dtype=jnp.float32) * s_in, 'bd': jnp.zeros((E, R), dtype=jnp.float32), 'Wu': jax.random.normal(ks[4], (E, R, D), dtype=jnp.float32) * s_r, 'bu': jnp.zeros((E, D), dtype=jnp.float32)}
    _L0_ffn_all = _L0_ffn_setup()
    _L0_ffn_in = {k: v for k, v in _L0_ffn_all.items() if k in ('Wr', 'br', 'Wd', 'bd', 'Wu', 'bu')}
    del _L0_ffn_all
    return {'x': x, 'ctx_512': ctx_512, 'L0_attn_Wq': _L0_attn_in['Wq'], 'L0_attn_Wk': _L0_attn_in['Wk'], 'L0_attn_Wv': _L0_attn_in['Wv'], 'L0_attn_Wb': _L0_attn_in['Wb'], 'L0_attn_bb': _L0_attn_in['bb'], 'L0_attn_Wo': _L0_attn_in['Wo'], 'L0_xattn_q_norm_w': _L0_xattn_in['q_norm_w'], 'L0_xattn_k_norm_w': _L0_xattn_in['k_norm_w'], 'L0_xattn_w_out': _L0_xattn_in['w_out'], 'L0_ffn_Wr': _L0_ffn_in['Wr'], 'L0_ffn_br': _L0_ffn_in['br'], 'L0_ffn_Wd': _L0_ffn_in['Wd'], 'L0_ffn_bd': _L0_ffn_in['bd'], 'L0_ffn_Wu': _L0_ffn_in['Wu'], 'L0_ffn_bu': _L0_ffn_in['bu']}

def reference(x, ctx_512, L0_attn_Wq, L0_attn_Wk, L0_attn_Wv, L0_attn_Wb, L0_attn_bb, L0_attn_Wo, L0_xattn_q_norm_w, L0_xattn_k_norm_w, L0_xattn_w_out, L0_ffn_Wr, L0_ffn_br, L0_ffn_Wd, L0_ffn_bd, L0_ffn_Wu, L0_ffn_bu):
    import jax
    import jax.numpy as jnp

    def _L0_attn_ref(hidden_states, Wq, Wk, Wv, Wb, bb, Wo):
        import jax, jax.numpy as jnp
        import numpy as np
        HID = 512
        H = 16
        D = HID // H
        THETA = 10000.0

        def _rope(q, k):
            T = q.shape[1]
            half = D // 2
            inv_freq = 1.0 / THETA ** (jnp.arange(half, dtype=jnp.float32) / half)
            ang = jnp.arange(T, dtype=jnp.float32)[:, None] * inv_freq[None, :]
            cos = jnp.cos(ang)[None, :, None, :]
            sin = jnp.sin(ang)[None, :, None, :]

            def rot(x):
                x1, x2 = (x[..., :half], x[..., half:])
                return jnp.concatenate([x1 * cos - x2 * sin, x2 * cos + x1 * sin], axis=-1)
            return (rot(q), rot(k))
        B, T, _ = hidden_states.shape
        scale = 1.0 / np.sqrt(D)
        q = (hidden_states @ Wq).reshape(B, T, H, D)
        k = (hidden_states @ Wk).reshape(B, T, H, D)
        v = (hidden_states @ Wv).reshape(B, T, H, D)
        beta = hidden_states @ Wb + bb
        q, k = _rope(q, k)
        s = jnp.einsum('bihd,bjhd->bhij', k, k) * scale
        idx = jnp.arange(T)
        strict = idx[:, None] > idx[None, :]
        s = jnp.where(strict, s, -jnp.inf)
        m = jnp.max(s, axis=-1, keepdims=True)
        e = jnp.exp(s - jnp.where(jnp.isfinite(m), m, 0.0))
        e = jnp.where(strict, e, 0.0)
        denom = jnp.sum(e, axis=-1, keepdims=True)
        p = e / jnp.where(denom == 0, 1.0, denom)
        L = p * beta.transpose(0, 2, 1)[..., None]
        A = L + jnp.eye(T, dtype=L.dtype)[None, None]
        u = jax.scipy.linalg.solve_triangular(A, v.transpose(0, 2, 1, 3), lower=True)
        sc = jnp.einsum('bihd,bjhd->bhij', q, k) * scale
        causal = idx[:, None] >= idx[None, :]
        sc = jnp.where(causal, sc, -jnp.inf)
        attn = jax.nn.softmax(sc, axis=-1)
        o = jnp.einsum('bhij,bhjd->bihd', attn, u).reshape(B, T, HID)
        return o @ Wo

    def _L0_xattn_ref(q, k, v, q_norm_w, k_norm_w, w_out):
        import jax, jax.numpy as jnp
        import numpy as np
        N_HEADS = 16
        N_KV_HEADS = 4
        ROPE_THETA = 10000.0
        EPS = 1e-05

        def _rms_norm(x, w):
            var = jnp.mean(x * x, axis=-1, keepdims=True)
            return x * jax.lax.rsqrt(var + EPS) * w

        def _rope_sin_cos(T, head_dim, dtype):
            inv_freq = 1.0 / ROPE_THETA ** (jnp.arange(0, head_dim, 2, dtype=jnp.float32) / head_dim)
            t = jnp.arange(T, dtype=jnp.float32)
            freqs = jnp.outer(t, inv_freq)
            emb = jnp.concatenate([freqs, freqs], -1)
            return (jnp.sin(emb).astype(dtype)[None, None], jnp.cos(emb).astype(dtype)[None, None])

        def _rotate_half(x):
            h = x.shape[-1] // 2
            x1, x2 = (x[..., :h], x[..., h:])
            return jnp.concatenate([-x2, x1], axis=-1)
        B, T, C = q.shape
        hd = C // N_HEADS
        g = N_HEADS // N_KV_HEADS
        q = _rms_norm(q, q_norm_w)
        k = _rms_norm(k, k_norm_w)
        q = q.reshape(B, T, N_HEADS, hd).transpose(0, 2, 1, 3)
        k = k.reshape(B, T, N_KV_HEADS, hd).transpose(0, 2, 1, 3)
        v = v.reshape(B, T, N_KV_HEADS, hd).transpose(0, 2, 1, 3)
        sin, cos = _rope_sin_cos(T, hd, q.dtype)
        q = q * cos + _rotate_half(q) * sin
        k = k * cos + _rotate_half(k) * sin
        qg = q.reshape(B, N_KV_HEADS, g, T, hd)
        scale = 1.0 / jnp.sqrt(jnp.asarray(hd, q.dtype))
        scores = jnp.einsum('bgnqd,bgkd->bgnqk', qg, k) * scale
        causal = jnp.tril(jnp.ones((T, T), bool))
        scores = jnp.where(causal, scores, jnp.asarray(-1e+30, scores.dtype))
        attn = jax.nn.softmax(scores, axis=-1)
        out = jnp.einsum('bgnqk,bgkd->bgnqd', attn, v)
        out = out.reshape(B, N_HEADS, T, hd).transpose(0, 2, 1, 3).reshape(B, T, C)
        return out @ w_out.T

    def _L0_ffn_ref(x, Wr, br, Wd, bd, Wu, bu):
        import jax, jax.numpy as jnp
        import numpy as np
        D = 512
        E = 8
        R = 16
        K = 2
        INIT_BONUS = 3.0
        ANNEAL_STEPS = 1250
        CURRENT_STEP = 1
        logits = jnp.einsum('btd,de->bte', x, Wr) + br
        progress = min(CURRENT_STEP / ANNEAL_STEPS, 1.0)
        bonus = INIT_BONUS * (1.0 - progress)
        logits = logits + bonus
        gates = jax.nn.softmax(logits, axis=-1)
        topk_vals, topk_idx = jax.lax.top_k(gates, K)
        topk_vals = topk_vals / topk_vals.sum(axis=-1, keepdims=True)
        w = (jax.nn.one_hot(topk_idx, E, dtype=x.dtype) * topk_vals[..., None]).sum(axis=-2)
        h = jax.nn.relu(jnp.einsum('btd,edr->betr', x, Wd) + bd[None, :, None, :])
        eo = jnp.einsum('betr,erd->betd', h, Wu) + bu[None, :, None, :]
        out = jnp.einsum('bte,betd->btd', w, eo)
        return out
    x = x + _L0_attn_ref(_layernorm(x, axis=-1), L0_attn_Wq, L0_attn_Wk, L0_attn_Wv, L0_attn_Wb, L0_attn_bb, L0_attn_Wo)
    x = x + _L0_xattn_ref(_layernorm(x, axis=-1), ctx_512, ctx_512, L0_xattn_q_norm_w, L0_xattn_k_norm_w, L0_xattn_w_out)
    x = x + _L0_ffn_ref(_layernorm(x, axis=-1), L0_ffn_Wr, L0_ffn_br, L0_ffn_Wd, L0_ffn_bd, L0_ffn_Wu, L0_ffn_bu)
    return x

_drawn_inputs = setup_inputs


def setup_inputs(seed=0):
    import zlib

    import numpy as np

    out = dict(_drawn_inputs(seed))
    spreads = {'L0_attn_bb': (0.0, 0.1),
     'L0_xattn_q_norm_w': (1.0, 0.2),
     'L0_xattn_k_norm_w': (1.0, 0.2),
     'L0_ffn_bd': (0.0, 0.1),
     'L0_ffn_bu': (0.0, 0.1)}
    factors = {}
    for name, (base, spread) in spreads.items():
        noise = np.random.default_rng([zlib.crc32(name.encode()), seed]).standard_normal(out[name].shape)
        drawn = base * np.exp(spread * noise) if base else spread * noise
        out[name] = jnp.asarray(drawn.astype(out[name].dtype))
    for name, factor in factors.items():
        out[name] = (out[name] * factor).astype(out[name].dtype)
    return out
```

```python
from contextlib import ExitStack

import numpy as np

import concourse.bass as bass
from concourse import mybir

F32 = mybir.dt.float32
BF16 = mybir.dt.bfloat16
ALU = mybir.AluOpType
ACT = mybir.ActivationFunctionType
AX = mybir.AxisListType

P = 128
D = 512
H = 16
DH = D // H
G = 4
CTX = G * DH
NC = D // P
HC = H // NC
NB = 4
Q = 32
NS = P // Q
E = 8
R = 16
EPS = 1e-5
THETA = 10000.0
BONUS = 3.0 * (1.0 - min(1 / 1250, 1.0))
NEG = -1e30
HH = H // 2
E_SLOTS = 8

A_USES, D_USES, S_USES = 61, 66, 48
A_NORM, A_V, A_KT, A_QT, A_CK = (0, 1, 8, 12), (2, 5, 9, 13), (3, 6, 10, 14), (4, 7, 11, 15), 40


def a_att(b, c): return 16 + NC * b + c
def a_u(s, f): return 32 + 2 * s + f
def a_mix(n): return 41 + n if n < NB else 45 + n
def a_xq(b): return 45 + b
def a_norm3(b): return 53 + b
def a_hw(b): return 57 + b


def d_low(b, c): return 12 + NC * b + c
def d_rhs(s, f): return 28 + 2 * (s - 1) + f
def d_proj(n): return 34 + n if n < NB else 42 + (NC + 1) * (n - NB)
def d_xatt(b, c): return 38 + (NC + 1) * b + c
def d_hid(b): return 58 + b
def d_ffn(b): return 62 + b


DVE_LINKS = 43
POOL_LINKS = 134


def constants():
    tok = (np.arange(P)[:, None] - Q * np.arange(NB)[None, :]) % P
    half = DH // 2
    inv = (1.0 / np.float32(THETA) ** (np.arange(half, dtype=np.float32) / np.float32(half))).astype(np.float32)
    ang = tok.astype(np.float32)[:, :, None] * inv
    root = np.float32(DH ** -0.25)
    cos, sin = np.cos(ang) * root, np.sin(ang) * root
    rope = np.stack([np.concatenate([cos, cos], -1), np.concatenate([-sin, sin], -1)], 2)
    earlier = tok[:, :, None] > tok.T[None, :, :]
    upto = tok[:, :, None] >= tok.T[None, :, :]
    mask = np.stack([np.where(earlier, 0.0, NEG), np.where(upto, 0.0, NEG)], 1)
    notfirst = np.where(tok == 0, 0.0, -1.0)
    before = np.tile((np.arange(E)[None, :] < np.arange(E)[:, None]).astype(np.float32)[None], (P, 1, 1))
    return (rope.astype(np.float32), mask.astype(np.float32), notfirst.astype(np.float32), before)


def pieces(b):
    if b == 0:
        return [(0, 0, P)]
    return [(0, Q * b, P - Q * b), (P - Q * b, 0, Q * b)]


def decoder_layer(nc, x, ctx_512, Wq, Wk, Wv, Wb, bb, Wo, qnw, knw, w_out, Wr, br, Wd, bd, Wu, bu, out):
    B = x.shape[0]
    TURNS = B // NB
    rope_c, mask_c, notfirst_c, before_c = constants()
    rope_d = nc.inline_tensor(rope_c, name="rope_c").ap()
    mask_d = nc.inline_tensor(mask_c, name="mask_c").ap()
    notfirst_d = nc.inline_tensor(notfirst_c, name="notfirst_c").ap()
    before_d = nc.inline_tensor(before_c, name="before_c").ap()
    blk_d = nc.dram_tensor("blk_d", [NB, NS, H, Q, Q], F32).ap()
    inv_d = nc.dram_tensor("inv_d", [NB, NS, H, Q, Q], F32).ap()

    with ExitStack() as stack:
        def sb(name, shape, dt=F32):
            return stack.enter_context(nc.sbuf_tensor(name, shape, dt))

        def sem(name):
            return stack.enter_context(nc.semaphore(name))

        wq = sb("wq", [P, NC, D]); wk = sb("wk", [P, NC, D]); wv = sb("wv", [P, NC, D])
        wb = sb("wb", [P, NC, H]); wo = sb("wo", [P, NC, D]); woutT = sb("woutT", [P, NC, D])
        wdr = sb("wdr", [P, NC, E * R + E]); wu = sb("wu", [P, D]); bu_s = sb("bu_s", [E, D])
        bb_s = sb("bb_s", [P, H]); qnw_s = sb("qnw_s", [P, D]); knw_s = sb("knw_s", [P, CTX])
        brb = sb("brb", [P, E]); bd_s = sb("bd_s", [P, E * R])
        rope = sb("rope", [P, NB, 2, DH]); masks = sb("masks", [P, 2, NB, P], BF16)
        notfirst = sb("notfirst", [P, NB]); before = sb("before", [P, E, E])
        ident = sb("ident", [P, P]); identb = sb("identb", [P, P], BF16)
        c_eps = sb("c_eps", [P, NB]); c_mhalf = sb("c_mhalf", [P, NB])
        c_1eps = sb("c_1eps", [P, NB]); c_eps2 = sb("c_eps2", [P, NB])

        xs = sb("xs", [P, NB, D]); ctx = sb("ctx", [P, NB, CTX])
        st6 = sb("st6", [P, NB, 6]); mv = sb("mv", [P, NB, 2]); va = sb("va", [P, NB]); rs = sb("rs", [P, NB])
        ct6 = sb("ct6", [P, NB, 6]); cmv = sb("cmv", [P, NB, 2]); cva = sb("cva", [P, NB]); crs = sb("crs", [P, NB])
        vb = sb("vb", [P, NB])
        work = sb("work", [P, 4 * D])
        xn = work[:, 0:2 * D].rearrange("p (a n) -> p a n", a=2)
        hT = work[:, 2 * D:4 * D].rearrange("p (a c j) -> p a c j", a=2, c=NC)
        blk = work[:, :].rearrange("p (a j i) -> p a j i", a=2, j=Q)
        tmp = work[:, 0:D].rearrange("p (a n) -> p a n", a=2)
        oT = hT
        tc = sb("tc", [P, 2, 2, D]); ts = sb("ts", [P, 2, D])
        outer = ts[:, 0, 0:(Q // 2) ** 2]
        ckn = tc[:, 1, 1, :].rearrange("p (b n) -> p b n", b=NB)
        cks = ts[:, 1, :].rearrange("p (b n) -> p b n", b=NB)
        ckr = sb("ckr", [P, NB, CTX])
        kT = sb("kT", [P, NB, NC, P]); qT = sb("qT", [P, NB, NC, P])
        inv = kT[:, :, :, :].rearrange("p b c j -> p (b c j)").rearrange("p (s h i) -> p s h i", s=NS, h=H)
        kbd = sb("kbd", [P, 2, NC, HC, P])
        kxbd = kbd[:, 0, :, :, :]
        beta = sb("beta", [P, NB, H]); nmax = sb("nmax", [P, 2, H]); den = sb("den", [P, 2, H])
        coef = sb("coef", [P, 2, H])
        prob = sb("prob", [P, E_SLOTS, HC, P])
        us = prob[:, 0:NB, :, :].rearrange("p b h j -> p b (h j)")
        lowT = sb("lowT", [P, NB, H, P]); attT = sb("attT", [P, NB, H, P])
        vst = sb("vst", [P, NS, D])
        h1 = vst[:, 0, :].rearrange("p (b n) -> p b n", b=NB)
        wpad = vst[:, 1, :].rearrange("p (b n) -> p b n", b=NB)
        hwT = vst[:, 2, 0:2 * P].rearrange("p (a j) -> p a j", a=2)
        wT = vst[:, 2, 2 * P:4 * P].rearrange("p (a j) -> p a j", a=2)
        cmp1 = vst[:, 3, 0:NB * E * E].rearrange("p (b e f) -> p b e f", b=NB, e=E)
        cmp2 = vst[:, 3, NB * E * E:2 * NB * E * E].rearrange("p (b e f) -> p b e f", b=NB, e=E)
        lg = sb("lg", [P, NB, E]); lmax = sb("lmax", [P, NB]); ex = sb("ex", [P, NB, E])
        rank = sb("rank", [P, NB, E])
        wsel = sb("wsel", [P, NB, E]); wsum = sb("wsum", [P, NB])

        bank = [stack.enter_context(nc.psum_tensor(f"bank{i}", [P, 512], F32)) for i in range(8)]
        ring_a, ring_d, ring_s = bank[0:3], bank[3:6], bank[6:8]
        a_full = sem("a_full"); a_read = sem("a_read"); d_full = sem("d_full"); d_read = sem("d_read")
        s_full = sem("s_full"); max_ready = sem("max_ready"); exp_done = sem("exp_done")
        loaded = sem("loaded"); mask_in = sem("mask_in"); table_done = sem("table_done"); pool_const = sem("pool_const")
        pool_step = sem("pool_step"); wout_full = sem("wout_full"); wout_done = sem("wout_done")
        x_in = [sem(f"x_in{b}") for b in range(NB)]; c_in = [sem(f"c_in{b}") for b in range(NB)]
        stats1 = sem("stats1"); rstd1 = sem("rstd1"); norm1 = sem("norm1")
        cstats = sem("cstats"); crstd = sem("crstd"); ck_rot = sem("ck_rot"); rot_done = sem("rot_done")
        stats2 = sem("stats2"); rstd2 = sem("rstd2"); xq_prod = sem("xq_prod"); xq_rot = sem("xq_rot")
        stats3 = sem("stats3"); rstd3 = sem("rstd3"); norm3 = sem("norm3")
        coef_low = sem("coef_low"); coef_x = sem("coef_x")
        scaled = [sem("scaled_low"), sem("scaled_att"), sem("scaled_x")]
        kbd_in = [sem("kbd_in0"), sem("kbd_in1")]
        blk_out = [sem(f"blk_out{b}") for b in range(NB)]; blk_in = [sem("blk_in0"), sem("blk_in1")]
        inv_done = sem("inv_done"); inv_out = [sem("inv_out0"), sem("inv_out1")]; inv_in = [sem("inv_in0"), sem("inv_in1")]
        u_zero = sem("u_zero"); tmp_ready = sem("tmp_ready")
        gate_max = sem("gate_max"); gate_exp = sem("gate_exp"); hw_ready = sem("hw_ready")
        dve_link = sem("dve_link"); pool_link = sem("pool_link"); stored = sem("stored"); turn_done = sem("turn_done")
        passed = {e: sem(f"passed_{e}") for e in ("sp", "pe", "dve", "pool")}
        N_LOADS = 36

        block = stack.enter_context(nc.Block())

        def heads(ap):
            return ap.rearrange("p (h d) -> p h d", d=DH)

        @block.sync
        def _(sp):
            sp.dma_start(lowT[:, 0, 0:2 * NB, :],
                         mask_d.rearrange("p a b j -> p (a b) j")).then_inc(mask_in, 16)
            for dst, src in ((wq, Wq), (wk, Wk), (wv, Wv), (wo, Wo), (wb, Wb)):
                sp.dma_start(dst[:, :, :], src.rearrange("(c p) n -> p c n", p=P)).then_inc(loaded, 16)
            for o in range(NC):
                for c in range(NC):
                    sp.dma_start(attT[:, 0, o * NC + c, :].rearrange("p (g d) -> p g d", g=G),
                                 w_out[o * P:(o + 1) * P, :].rearrange("p (g c d) -> p c g d", g=G, c=NC)[:, c, :, :]).then_inc(loaded, 16)
            for c in range(NC):
                sp.dma_start(wdr[:, c, 0:E * R].rearrange("p (e r) -> p e r", e=E),
                             Wd[:, c * P:(c + 1) * P, :].rearrange("e p r -> p e r")).then_inc(loaded, 16)
            sp.dma_start(wdr[:, :, E * R:], Wr.rearrange("(c p) e -> p c e", p=P)).then_inc(loaded, 16)
            sp.dma_start(wu[:, :], Wu.rearrange("e r d -> (e r) d")).then_inc(loaded, 16)
            sp.dma_start(bu_s[:, :], bu).then_inc(loaded, 16)
            sp.dma_start(bb_s[:, :], bb.partition_broadcast(P)).then_inc(loaded, 16)
            sp.dma_start(qnw_s[:, :], qnw.partition_broadcast(P)).then_inc(loaded, 16)
            sp.dma_start(knw_s[:, :], knw.partition_broadcast(P)).then_inc(loaded, 16)
            sp.dma_start(brb[:, :], br.partition_broadcast(P)).then_inc(loaded, 16)
            sp.dma_start(bd_s[:, :], bd.rearrange("e r -> (e r)").partition_broadcast(P)).then_inc(loaded, 16)
            sp.dma_start(rope[:, :, :, :], rope_d).then_inc(loaded, 16)
            sp.dma_start(notfirst[:, :], notfirst_d).then_inc(loaded, 16)
            sp.dma_start(before[:, :, :], before_d).then_inc(loaded, 16)
            with sp.Fori(0, TURNS) as t:
                for b in range(NB):
                    for t0, p0, n in pieces(b):
                        sp.dma_start(xs[p0:p0 + n, b, :],
                                     x[bass.ds(t * NB + b, 1), t0:t0 + n, :].rearrange("o t d -> (o t) d")).then_inc(x_in[b], 16)
                    for t0, p0, n in pieces(b):
                        sp.dma_start(ctx[p0:p0 + n, b, :],
                                     ctx_512[bass.ds(t * NB + b, 1), t0:t0 + n, :].rearrange("o t d -> (o t) d")).then_inc(c_in[b], 16)

                def spread_keys(n):
                    b = n % NB
                    sp.wait_ge(a_read, t * A_USES + A_KT[b] + 1)
                    sp.nop().then_inc(passed["sp"], 1)
                    if n >= 2:
                        sp.wait_ge(s_full, t * S_USES + NC * (n - 1))
                        sp.nop().then_inc(passed["sp"], 1)
                    for r in range(HC):
                        sp.dma_start(kbd[Q * r:Q * r + Q, n % 2, :, r, :], kT[Q * r:Q * r + Q, b, :, :]).then_inc(kbd_in[n % 2], 16)

                def blocks_out(b):
                    sp.wait_ge(d_read, t * D_USES + d_low(b, NC - 1) + 1)
                    sp.nop().then_inc(passed["sp"], 1)
                    for s in range(NS):
                        q = Q * ((s + b) % NS)
                        sp.dma_start(blk_d[b, s].rearrange("h j i -> j h i"),
                                     lowT[q:q + Q, b, :, q:q + Q]).then_inc(blk_out[b], 16)

                def blocks_in(g):
                    for b in (2 * g, 2 * g + 1):
                        sp.wait_ge(blk_out[b], 16 * NS * (t + 1))
                        sp.nop().then_inc(passed["sp"], 1)
                    sp.dma_start(blk[:, g, :, :].rearrange("p j i -> p (j i)"),
                                 blk_d[2 * g:2 * g + 2].rearrange("b s h j i -> (b s h) (j i)")).then_inc(blk_in[g], 16)

                def inverses_out(g):
                    sp.wait_ge(inv_done, t * 2 + g + 1)
                    sp.nop().then_inc(passed["sp"], 1)
                    sp.dma_start(inv_d[2 * g:2 * g + 2].rearrange("b s h j i -> (b s h) (j i)"),
                                 blk[:, g, :, :].rearrange("p j i -> p (j i)")).then_inc(inv_out[g], 16)
                    sp.wait_ge(inv_out[g], 16 * (t + 1))
                    sp.nop().then_inc(passed["sp"], 1)
                    for b in (2 * g, 2 * g + 1):
                        for s in range(NS):
                            q = Q * ((s + b) % NS)
                            sp.dma_start(inv[q:q + Q, s, :, :], inv_d[b, s].rearrange("h j i -> j h i")).then_inc(inv_in[g], 16)

                spread_keys(0); spread_keys(1)
                spread_keys(2)
                blocks_out(0)
                spread_keys(3)
                blocks_out(1)
                blocks_in(0)
                spread_keys(4)
                blocks_out(2)
                spread_keys(5)
                blocks_out(3)
                blocks_in(1)
                spread_keys(6); spread_keys(7)
                inverses_out(0); inverses_out(1)
                for b in range(NB):
                    sp.wait_ge(d_read, t * D_USES + d_ffn(b) + 1)
                    sp.nop().then_inc(passed["sp"], 1)
                    for t0, p0, n in pieces(b):
                        sp.dma_start(out[bass.ds(t * NB + b, 1), t0:t0 + n, :].rearrange("o t d -> (o t) d"),
                                     xs[p0:p0 + n, b, :]).then_inc(stored, 16)
                sp.wait_ge(stored, (t + 1) * 16 * (2 * NB - 1))
                sp.nop().then_inc(passed["sp"], 1)
                sp.nop().then_inc(turn_done, 1)
                sp.wait_ge(turn_done, (t + 1) * 5)
                sp.nop().then_inc(passed["sp"], 1)

        @block.tensor
        def _(pe):
            pe.wait_ge(pool_const, 1)
            pe.wait_ge(loaded, 16 * N_LOADS)
            for c in range(NC):
                if c >= 2:
                    pe.wait_ge(wout_done, c - 1)
                for o in range(NC):
                    mm = pe.transpose(ring_a[c % 2][:, o * P:(o + 1) * P], attT[:, 0, o * NC + c, :], ident[:, :])
                mm.then_inc(wout_full, 1)
            pe.wait_ge(wout_done, NC)
            pe.wait_ge(table_done, 4)
            with pe.Fori(0, TURNS) as t:
                uses = {"a": 0, "d": 0, "s": 0}

                def fill_a():
                    n = uses["a"]
                    uses["a"] += 1
                    if n >= 3:
                        pe.wait_ge(a_read, t * A_USES + n - 2)
                    return ring_a[n % 3]

                def fill_d():
                    n = uses["d"]
                    uses["d"] += 1
                    if n >= 3:
                        pe.wait_ge(d_read, t * D_USES + n - 2)
                    return ring_d[n % 3]

                def fill_s():
                    n = uses["s"]
                    uses["s"] += 1
                    if n >= 2:
                        pe.wait_ge(exp_done, t * S_USES + n - 1)
                    return ring_s[n % 2]

                def rows_T(src):
                    ps = fill_a()
                    for c in range(NC):
                        mm = pe.transpose(ps[:, c * P:(c + 1) * P], src(c), ident[:, :])
                    mm.then_inc(a_full, 1)

                def norm_T(b):
                    pe.wait_ge(norm1, t * NB + b + 1)
                    rows_T(lambda c: xn[:, b % 2, c * P:(c + 1) * P])

                def project(b):
                    pe.wait_ge(a_read, t * A_USES + A_NORM[b] + 1)
                    for w, fill, full in ((wv, fill_a, a_full), (wk, fill_d, d_full), (wq, fill_d, d_full), (wb, fill_d, d_full)):
                        ps = fill()
                        n = w.shape[2]
                        for c in range(NC):
                            mm = pe.matmul(ps[:, 0:n], hT[:, b % 2, c, :], w[:, c, :], start=(c == 0), stop=(c == NC - 1))
                        mm.then_inc(full, 1)

                def rotated_T(b):
                    for kq in range(2):
                        pe.wait_ge(rot_done, t * 2 * NB + 2 * b + kq + 1)
                        rows_T(lambda c: tc[:, b % 2, kq, c * P:(c + 1) * P])

                def scores(stat, keys, kind, b):
                    for c in range(NC):
                        ps = fill_s()
                        pe.matmul(ps[:, :], stat(c), keys(c), start=True, stop=False)
                        pe.matmul(ps[:, :].rearrange("p (h j) -> p h j", h=HC), identb[:, :],
                                  masks[:, kind, b, :].unsqueeze(1).broadcast_to([P, HC, P]),
                                  start=False, stop=True).then_inc(s_full, 1)

                def probs_T(kind, b, fill, full):
                    for c in range(NC):
                        pe.wait_ge(scaled[kind], t * NB * NC + b * NC + c + 1)
                        ps = fill()
                        slot = ((kind * NB + b) * NC + c) % E_SLOTS
                        for r in range(HC):
                            mm = pe.transpose(ps[:, r * P:(r + 1) * P], prob[:, slot, r, :], ident[:, :])
                        mm.then_inc(full, 1)

                def key_scores(b):
                    pe.wait_ge(kbd_in[b % 2], 16 * HC * (t * 4 + b // 2 + 1))
                    scores(lambda c: kT[:, b, c, :], lambda c: kbd[:, b % 2, c, :, :], 0, b)

                def query_scores(b):
                    pe.wait_ge(kbd_in[b % 2], 16 * HC * (t * 4 + 2 + b // 2 + 1))
                    pe.wait_ge(a_read, t * A_USES + A_QT[b] + 1)
                    scores(lambda c: qT[:, b, c, :], lambda c: kbd[:, b % 2, c, :, :], 1, b)

                norm_T(0); norm_T(1); project(0); rotated_T(0); project(1); rotated_T(1)
                for b in range(NB):
                    if b + 2 < NB:
                        norm_T(b + 2)
                    key_scores(b)
                    if b + 2 < NB:
                        project(b + 2)
                    if b >= 1:
                        probs_T(0, b - 1, fill_d, d_full)
                    if b + 2 < NB:
                        rotated_T(b + 2)
                query_scores(0)
                probs_T(0, NB - 1, fill_d, d_full)
                for b in range(1, NB):
                    query_scores(b)
                    probs_T(1, b - 1, fill_a, a_full)
                probs_T(1, NB - 1, fill_a, a_full)

                pe.wait_ge(d_read, t * D_USES + d_low(NB - 1, NC - 1) + 1)
                pe.wait_ge(u_zero, t + 1)
                for g in range(2):
                    pe.wait_ge(inv_in[g], 16 * 2 * NS * (t + 1))
                for s in range(NS):
                    for f in range(2 if s > 0 else 0):
                        pe.wait_ge(a_read, t * A_USES + a_u(s - 1, f) + 1)
                        ps = fill_d()
                        for h in range(f * HH, f * HH + HH):
                            for b in range(NB):
                                q = Q * ((s + b) % NS)
                                mm = pe.matmul(ps[q:q + Q, (h % HH) * DH:(h % HH + 1) * DH], lowT[:, b, h, q:q + Q],
                                               us[:, b, h * DH:(h + 1) * DH], start=True, stop=True)
                        mm.then_inc(d_full, 1)
                    for f in range(2):
                        if s > 0:
                            pe.wait_ge(tmp_ready, t * 2 * (NS - 1) + 2 * (s - 1) + f + 1)
                        ps = fill_a()
                        pe.nop().then_inc(passed["pe"], 1)
                        for h in range(f * HH, f * HH + HH):
                            for b in range(NB):
                                q = Q * ((s + b) % NS)
                                rhs = tmp[q:q + Q, f, (h % HH) * DH:(h % HH + 1) * DH] if s > 0 else vst[q:q + Q, 0, h * DH:(h + 1) * DH]
                                mm = pe.matmul(ps[q:q + Q, (h % HH) * DH:(h % HH + 1) * DH], inv[q:q + Q, s, h, :], rhs, start=True, stop=True)
                        mm.then_inc(a_full, 1)

                def mix(vals, b):
                    ps = fill_a()
                    for c in range(NC):
                        for r in range(HC):
                            mm = pe.matmul(ps[Q * r:Q * r + Q, c * P:(c + 1) * P], vals(c, r), attT[:, b, c * HC + r, :], start=True, stop=True)
                    mm.then_inc(a_full, 1)

                def out_proj(w, n):
                    pe.wait_ge(a_read, t * A_USES + a_mix(n) + 1)
                    ps = fill_d()
                    for c in range(NC):
                        mm = pe.matmul(ps[:, :], oT[:, n % 2, c, :], w[:, c, :], start=(c == 0), stop=(c == NC - 1))
                    mm.then_inc(d_full, 1)

                pe.wait_ge(ck_rot, t + 1)
                rows_T(lambda b: ckr[:, b, :])
                pe.wait_ge(a_read, t * A_USES + a_u(NS - 1, 1) + 1)
                for b in range(NB):
                    mix(lambda c, r: us[:, b, (c * HC + r) * DH:(c * HC + r + 1) * DH], b)
                    if b >= 1:
                        out_proj(wo, b - 1)
                out_proj(wo, NB - 1)

                def xq_rows_T(b):
                    pe.wait_ge(xq_rot, t * NB + b + 1)
                    rows_T(lambda c: tc[:, b % 2, 1, c * P:(c + 1) * P])

                xq_rows_T(0); xq_rows_T(1)
                for b in range(NB + 1):
                    if b < NB:
                        pe.wait_ge(a_read, t * A_USES + a_xq(b) + 1)
                        scores(lambda c: qT[:, b, c, :], lambda c: kxbd[:, b, :, :], 1, b)
                    if b + 2 < NB:
                        xq_rows_T(b + 2)
                    if b >= 1:
                        probs_T(2, b - 1, fill_d, d_full)
                        pe.wait_ge(d_read, t * D_USES + d_xatt(b - 1, NC - 1) + 1)
                        mix(lambda c, r: ctx[:, b - 1, r * DH:(r + 1) * DH], b - 1)
                        out_proj(woutT, NB + b - 1)

                for b in range(NB):
                    pe.wait_ge(norm3, t * NB + b + 1)
                    rows_T(lambda c: xn[:, b % 2, c * P:(c + 1) * P])
                    pe.wait_ge(a_read, t * A_USES + a_norm3(b) + 1)
                    ps = fill_d()
                    for c in range(NC):
                        mm = pe.matmul(ps[:, 0:E * R + E], hT[:, b % 2, c, :], wdr[:, c, :], start=(c == 0), stop=(c == NC - 1))
                    mm.then_inc(d_full, 1)
                for b in range(NB):
                    pe.wait_ge(hw_ready, t * NB + b + 1)
                    ps = fill_a()
                    pe.transpose(ps[:, 0:P], h1[:, b, :], ident[:, :])
                    pe.transpose(ps[:, P:2 * P], wpad[:, b, :], ident[:, :]).then_inc(a_full, 1)
                    pe.wait_ge(a_read, t * A_USES + a_hw(b) + 1)
                    ps = fill_d()
                    pe.matmul(ps[:, :], hwT[:, b % 2, :], wu[:, :], start=True, stop=False)
                    pe.matmul(ps[:, :], wT[0:E, b % 2, :], bu_s[:, :], start=False, stop=True).then_inc(d_full, 1)
                assert uses == {"a": A_USES, "d": D_USES, "s": S_USES}, uses
                pe.wait_ge(d_read, (t + 1) * D_USES)
                pe.nop().then_inc(turn_done, 1)
                pe.wait_ge(turn_done, (t + 1) * 5)

        @block.scalar
        def _(act):
            for c in range(NC):
                act.wait_ge(wout_full, c + 1)
                act.activation(woutT[:, c, :], ring_a[c % 2][:, :], ACT.Copy).then_inc(wout_done, 1)
            with act.Fori(0, TURNS) as t:
                def copy_out(n, dst, cols=512):
                    act.wait_ge(a_full, t * A_USES + n + 1)
                    act.activation(dst, ring_a[n % 3][:, 0:cols], ACT.Copy).then_inc(a_read, 1)

                def flat(ap):
                    return ap.rearrange("p c j -> p (c j)")

                def norm_out(b):
                    if b >= 2:
                        act.wait_ge(d_full, t * D_USES + 3 * (b - 2) + 3)
                    copy_out(A_NORM[b], flat(hT[:, b % 2, :, :]))

                def values_out(b):
                    n = A_V[b]
                    act.wait_ge(a_full, t * A_USES + n + 1)
                    for s in range(NS):
                        q = Q * ((s + b) % NS)
                        ins = act.activation(vst[q:q + Q, s, :], ring_a[n % 3][q:q + Q, :], ACT.Copy)
                    ins.then_inc(a_read, 1)

                def exps(n):
                    for c in range(NC):
                        i = n * NC + c
                        act.wait_ge(max_ready, t * S_USES + i + 1)
                        if i >= E_SLOTS:
                            m = n - 2
                            if m < NB:
                                act.wait_ge(d_full, t * D_USES + d_low(m, c) + 1)
                            elif m < 2 * NB:
                                act.wait_ge(a_full, t * A_USES + a_att(m - NB, c) + 1)
                            else:
                                act.wait_ge(d_full, t * D_USES + d_xatt(m - 2 * NB, c) + 1)
                        for r in range(HC):
                            h = c * HC + r
                            ins = act.activation(prob[:, i % E_SLOTS, r, :], ring_s[i % 2][:, r * P:(r + 1) * P], ACT.Exp,
                                                 bias=nmax[:, n % 2, h:h + 1], accum_out=den[:, n % 2, h:h + 1])
                        ins.then_inc(exp_done, 1)

                norm_out(0); norm_out(1)
                for b in range(2):
                    values_out(b)
                    copy_out(A_KT[b], flat(kT[:, b, :, :]))
                    copy_out(A_QT[b], flat(qT[:, b, :, :]))
                for b in range(NB):
                    if b + 2 < NB:
                        norm_out(b + 2)
                    exps(b)
                    if b + 2 < NB:
                        values_out(b + 2)
                        copy_out(A_KT[b + 2], flat(kT[:, b + 2, :, :]))
                        copy_out(A_QT[b + 2], flat(qT[:, b + 2, :, :]))
                exps(NB)
                for b in range(1, NB + 1):
                    if b < NB:
                        exps(NB + b)
                    for c in range(NC):
                        copy_out(a_att(b - 1, c), flat(attT[:, b - 1, c * HC:(c + 1) * HC, :]))
                for s in range(NS):
                    for f in range(2):
                        n = a_u(s, f)
                        act.wait_ge(a_full, t * A_USES + n + 1)
                        for b in range(NB):
                            q = Q * ((s + b) % NS)
                            ins = act.activation(us[q:q + Q, b, f * HH * DH:(f + 1) * HH * DH], ring_a[n % 3][q:q + Q, 0:HH * DH], ACT.Copy)
                        ins.then_inc(a_read, 1)

                act.wait_ge(a_full, t * A_USES + A_CK + 1)
                for g in range(G):
                    ins = act.activation(kxbd[Q * g:Q * g + Q, :, g, :],
                                         ring_a[A_CK % 3][Q * g:Q * g + Q, :].rearrange("p (b j) -> p b j", b=NB), ACT.Copy)
                ins.then_inc(a_read, 1)

                def mix_out(n):
                    if n >= 2:
                        act.wait_ge(d_full, t * D_USES + d_proj(n - 2) + 1)
                    copy_out(a_mix(n), flat(oT[:, n % 2, :, :]))

                for b in range(NB):
                    mix_out(b)
                copy_out(a_xq(0), flat(qT[:, 0, :, :])); copy_out(a_xq(1), flat(qT[:, 1, :, :]))
                for b in range(NB + 1):
                    if b < NB:
                        exps(2 * NB + b)
                    if b + 2 < NB:
                        copy_out(a_xq(b + 2), flat(qT[:, b + 2, :, :]))
                    if b >= 1:
                        mix_out(NB + b - 1)
                for b in range(NB):
                    if b >= 2:
                        act.wait_ge(d_full, t * D_USES + d_hid(b - 2) + 1)
                    copy_out(a_norm3(b), flat(hT[:, b % 2, :, :]))
                act.wait_ge(gate_max, t + 1)
                act.activation(ex[:, :, :], lg[:, :, :], ACT.Exp).then_inc(gate_exp, 1)
                for b in range(NB):
                    n = a_hw(b)
                    act.wait_ge(a_full, t * A_USES + n + 1)
                    if b >= 2:
                        act.wait_ge(d_full, t * D_USES + d_ffn(b - 2) + 1)
                    act.activation(hwT[:, b % 2, :], ring_a[n % 3][:, 0:P], ACT.Copy)
                    act.activation(wT[:, b % 2, :], ring_a[n % 3][:, P:2 * P], ACT.Copy).then_inc(a_read, 1)
                act.wait_ge(a_read, (t + 1) * A_USES)
                act.nop().then_inc(turn_done, 1)
                act.wait_ge(turn_done, (t + 1) * 5)

        @block.vector
        def _(dve):
            dve.memset(kbd[:, :, :, :, :], 0.0).then_inc(table_done, 1)
            dve.wait_ge(mask_in, 16)
            dve.tensor_copy(masks[:, :, :, :].rearrange("p a b j -> p (a b) j"), lowT[:, 0, 0:2 * NB, :]).then_inc(table_done, 1)
            dve.wait_ge(pool_const, 1)
            dve.tensor_copy(identb[:, :], ident[:, :]).then_inc(table_done, 1)
            dve.wait_ge(loaded, 16 * N_LOADS)
            dve.tensor_scalar(brb[:, :], brb[:, :], BONUS, None, ALU.add).then_inc(table_done, 1)
            dve.wait_ge(table_done, 4)
            with dve.Fori(0, TURNS) as t:
                links = [0]

                def link(ins):
                    links[0] += 1
                    ins.then_inc(dve_link, 1)
                    dve.wait_ge(dve_link, t * DVE_LINKS + links[0])

                def from_d(n):
                    dve.wait_ge(d_full, t * D_USES + n + 1)
                    return ring_d[n % 3]

                def swapped(ap):
                    return ap.rearrange("p (h a d) -> p h a d", a=2, d=DH // 2)[:, :, ::-1, :]

                def table(b, k, n):
                    return rope[:, b, k, :].unsqueeze(1).broadcast_to([P, n, DH])

                def table2(b, k, n):
                    return rope[:, b, k, :].rearrange("p (a d) -> p a d", a=2).unsqueeze(1).broadcast_to([P, n, 2, DH // 2])

                def halves(ap):
                    return ap.rearrange("p (h a d) -> p h a d", a=2, d=DH // 2)

                for b in range(NB):
                    dve.wait_ge(x_in[b], 16 * len(pieces(b)) * (t + 1))
                    link(dve.bn_stats(st6[:, b, :], xs[:, b, :]))
                    dve.nop().then_inc(passed["dve"], 1)
                    dve.bn_aggr(mv[:, b, :], st6[:, b, :]).then_inc(stats1, 1)

                def norm(b, r, done):
                    dve.tensor_scalar(xn[:, b % 2, :], xs[:, b, :], mv[:, b, 0:1], r[:, b:b + 1],
                                      ALU.subtract, ALU.mult).then_inc(done, 1)

                dve.wait_ge(rstd1, t + 1)
                norm(0, rs, norm1); norm(1, rs, norm1)

                for b in range(NB):
                    dve.wait_ge(c_in[b], 16 * len(pieces(b)) * (t + 1))
                    link(dve.bn_stats(ct6[:, b, :], ctx[:, b, :]))
                    dve.nop().then_inc(passed["dve"], 1)
                    dve.bn_aggr(cmv[:, b, :], ct6[:, b, :]).then_inc(cstats, 1)
                dve.wait_ge(crstd, t + 1)
                for b in range(NB):
                    ins = dve.scalar_tensor_tensor(ckn[:, b, :], ctx[:, b, :], crs[:, b:b + 1], knw_s[:, :], ALU.mult, ALU.mult)
                link(ins)
                for b in range(NB):
                    dve.tensor_tensor(heads(ckr[:, b, :]), heads(ckn[:, b, :]), table(b, 0, G), ALU.mult)
                    ins = dve.tensor_tensor(halves(cks[:, b, :]), swapped(ckn[:, b, :]), table2(b, 1, G), ALU.mult)
                link(ins)
                dve.tensor_tensor(ckr[:, :, :], ckr[:, :, :], cks[:, :, :], ALU.add).then_inc(ck_rot, 1)

                def rope_products(b):
                    if b >= 1:
                        dve.wait_ge(rot_done, t * 2 * NB + 2 * b)
                    else:
                        dve.wait_ge(ck_rot, t + 1)
                    if b >= 2:
                        dve.wait_ge(a_read, t * A_USES + A_QT[b - 2] + 1)
                    for kq in range(2):
                        ps = from_d(3 * b + kq)
                        dve.tensor_tensor(heads(tc[:, b % 2, kq, :]), heads(ps[:, :]), table(b, 0, H), ALU.mult)
                        dve.tensor_tensor(halves(ts[:, kq, :]), swapped(ps[:, :]), table2(b, 1, H), ALU.mult).then_inc(d_read, 1)
                    ps = from_d(3 * b + 2)
                    dve.tensor_tensor(beta[:, b, :], ps[:, 0:H], bb_s[:, :], ALU.add).then_inc(d_read, 1)

                def row_max(n):
                    for c in range(NC):
                        i = n * NC + c
                        dve.wait_ge(s_full, t * S_USES + i + 1)
                        if n >= 2:
                            dve.wait_ge(exp_done, t * S_USES + (n - 2) * NC + c + 1)
                        dve.tensor_reduce(nmax[:, n % 2, c * HC:(c + 1) * HC], ring_s[i % 2][:, :].rearrange("p (h j) -> p h j", h=HC),
                                          AX.X, ALU.max, negate=True).then_inc(max_ready, 1)

                def low_factors(b):
                    dve.wait_ge(exp_done, t * S_USES + (b + 1) * NC)
                    if b >= 2:
                        dve.wait_ge(scaled[0], t * NB * NC + (b - 1) * NC)
                    link(dve.reciprocal(coef[:, b % 2, :], den[:, b % 2, :]))
                    dve.scalar_tensor_tensor(coef[:, b % 2, :], coef[:, b % 2, :], notfirst[:, b:b + 1], beta[:, b, :],
                                             ALU.mult, ALU.mult).then_inc(coef_low, 1)

                def low_out(b):
                    for c in range(NC):
                        ps = from_d(d_low(b, c))
                        dve.tensor_copy(lowT[:, b, c * HC:(c + 1) * HC, :].rearrange("p h i -> p (h i)"), ps[:, :]).then_inc(d_read, 1)

                rope_products(0); rope_products(1)
                for b in range(NB):
                    if b + 2 < NB:
                        dve.wait_ge(a_read, t * A_USES + A_NORM[b] + 1)
                        norm(b + 2, rs, norm1)
                    row_max(b)
                    if b + 2 < NB:
                        rope_products(b + 2)
                    low_factors(b)
                    if b >= 1:
                        low_out(b - 1)

                def att_scale(b):
                    n = NB + b
                    dve.wait_ge(exp_done, t * S_USES + (n + 1) * NC)
                    link(dve.reciprocal(coef[:, n % 2, :], den[:, n % 2, :]))
                    for c in range(NC):
                        sl = prob[:, (n * NC + c) % E_SLOTS, :, :]
                        dve.tensor_tensor(sl, sl, coef[:, n % 2, c * HC:(c + 1) * HC].unsqueeze(2).broadcast_to([P, HC, P]),
                                          ALU.mult).then_inc(scaled[1], 1)

                row_max(NB)
                low_out(NB - 1)
                for b in range(1, NB + 1):
                    if b < NB:
                        row_max(NB + b)
                    att_scale(b - 1)

                dve.wait_ge(a_read, t * A_USES + A_V[NB - 1] + 1)
                for s in range(1, NS):
                    for f in range(2):
                        ps = from_d(d_rhs(s, f))
                        dve.tensor_tensor(tmp[:, f, :], ps[:, 0:HH * DH], vst[:, s, f * HH * DH:(f + 1) * HH * DH], ALU.add).then_inc(tmp_ready, 1)
                        dve.wait_ge(tmp_ready, t * 2 * (NS - 1) + 2 * (s - 1) + f + 1)
                        dve.nop().then_inc(d_read, 1)

                def add_out(n, stats):
                    b = n % NB
                    ps = from_d(d_proj(n))
                    dve.tensor_tensor(xs[:, b, :], ps[:, :], xs[:, b, :], ALU.add).then_inc(d_read, 1)
                    dve.wait_ge(d_read, t * D_USES + d_proj(n) + 1)
                    link(dve.bn_stats(st6[:, b, :], xs[:, b, :]))
                    dve.nop().then_inc(passed["dve"], 1)
                    dve.bn_aggr(mv[:, b, :], st6[:, b, :]).then_inc(stats, 1)

                def cross_queries(b):
                    dve.wait_ge(rstd2, t * NB + b + 1)
                    if b >= 1:
                        dve.wait_ge(xq_rot, t * NB + b)
                    link(dve.tensor_scalar(xn[:, b % 2, :], xs[:, b, :], mv[:, b, 0:1], rs[:, b:b + 1], ALU.subtract, ALU.mult))
                    link(dve.tensor_tensor(xn[:, b % 2, :], xn[:, b % 2, :], qnw_s[:, :], ALU.mult))
                    dve.tensor_tensor(heads(tc[:, b % 2, 0, :]), heads(xn[:, b % 2, :]), table(b, 0, H), ALU.mult)
                    dve.tensor_tensor(halves(ts[:, 0, :]), swapped(xn[:, b % 2, :]), table2(b, 1, H), ALU.mult).then_inc(xq_prod, 1)

                add_out(0, stats2); add_out(1, stats2); cross_queries(0)
                add_out(2, stats2); cross_queries(1); add_out(3, stats2)
                for b in range(NB + 1):
                    if b < NB:
                        row_max(2 * NB + b)
                    if b + 2 < NB:
                        cross_queries(b + 2)
                    if b < NB:
                        n = 2 * NB + b
                        dve.wait_ge(exp_done, t * S_USES + (n + 1) * NC)
                        if b >= 2:
                            dve.wait_ge(scaled[2], t * NB * NC + (b - 1) * NC)
                        dve.reciprocal(coef[:, n % 2, :], den[:, n % 2, :]).then_inc(coef_x, 1)
                    if b >= 1:
                        for c in range(NC):
                            ps = from_d(d_xatt(b - 1, c))
                            dve.tensor_copy(attT[:, b - 1, c * HC:(c + 1) * HC, :].rearrange("p h i -> p (h i)"), ps[:, :]).then_inc(d_read, 1)
                        add_out(NB + b - 1, stats3)

                def hidden_out(b):
                    ps = from_d(d_hid(b))
                    dve.tensor_tensor(h1[:, b, :], ps[:, 0:E * R], bd_s[:, :], ALU.add)
                    dve.tensor_tensor(lg[:, b, :], ps[:, E * R:E * R + E], brb[:, :], ALU.add).then_inc(d_read, 1)

                for b in range(NB):
                    dve.wait_ge(rstd3, t * NB + b + 1)
                    if b >= 2:
                        dve.wait_ge(a_read, t * A_USES + a_norm3(b - 2) + 1)
                    norm(b, rs, norm3)
                    if b >= 1:
                        hidden_out(b - 1)
                hidden_out(NB - 1)

                dve.wait_ge(d_read, t * D_USES + d_hid(NB - 1) + 1)
                link(dve.tensor_reduce(lmax[:, :], lg[:, :, :], AX.X, ALU.max))
                dve.tensor_tensor(lg[:, :, :], lg[:, :, :], lmax[:, :].unsqueeze(2).broadcast_to([P, NB, E]), ALU.subtract).then_inc(gate_max, 1)
                dve.wait_ge(gate_exp, t + 1)
                mine = ex[:, :, :].unsqueeze(3).broadcast_to([P, NB, E, E])
                other = ex[:, :, :].unsqueeze(2).broadcast_to([P, NB, E, E])
                dve.tensor_tensor(cmp1[:, :, :, :], other, mine, ALU.is_gt)
                link(dve.tensor_tensor(cmp2[:, :, :, :], other, mine, ALU.is_equal))
                link(dve.tensor_tensor(cmp2[:, :, :, :].rearrange("p b e f -> p b (e f)"), cmp2[:, :, :, :].rearrange("p b e f -> p b (e f)"),
                                       before[:, :, :].rearrange("p e f -> p (e f)").unsqueeze(1).broadcast_to([P, NB, E * E]), ALU.mult))
                link(dve.tensor_tensor(cmp1[:, :, :, :], cmp1[:, :, :, :], cmp2[:, :, :, :], ALU.add))
                link(dve.tensor_reduce(rank[:, :, :], cmp1[:, :, :, :], AX.X, ALU.add))
                link(dve.scalar_tensor_tensor(wsel[:, :, :], rank[:, :, :], 2.0, ex[:, :, :], ALU.is_lt, ALU.mult))
                link(dve.tensor_reduce(wsum[:, :], wsel[:, :, :], AX.X, ALU.add))
                link(dve.reciprocal(wsum[:, :], wsum[:, :]))
                link(dve.tensor_tensor(wpad[:, :, 0:E], wsel[:, :, :], wsum[:, :].unsqueeze(2).broadcast_to([P, NB, E]), ALU.mult))
                for b in range(NB):
                    hb = h1[:, b, :].rearrange("p (e r) -> p e r", e=E)
                    dve.scalar_tensor_tensor(hb, hb, 0.0, wpad[:, b, 0:E].unsqueeze(2).broadcast_to([P, E, R]),
                                             ALU.max, ALU.mult).then_inc(hw_ready, 1)
                for b in range(NB):
                    ps = from_d(d_ffn(b))
                    dve.tensor_tensor(xs[:, b, :], ps[:, :], xs[:, b, :], ALU.add).then_inc(d_read, 1)
                assert links[0] == DVE_LINKS, links
                dve.wait_ge(d_read, (t + 1) * D_USES)
                dve.nop().then_inc(turn_done, 1)
                dve.wait_ge(turn_done, (t + 1) * 5)

        @block.gpsimd
        def _(pool):
            pool.memset(ident[:, :], 0.0).then_inc(pool_step, 1)
            pool.memset(c_mhalf[:, :], -0.5).then_inc(pool_step, 1)
            pool.memset(c_eps[:, :], EPS).then_inc(pool_step, 1)
            pool.memset(c_1eps[:, :], 1.0 + EPS).then_inc(pool_step, 1)
            pool.memset(c_eps2[:, :], EPS * EPS).then_inc(pool_step, 1)
            pool.wait_ge(pool_step, 5)
            pool.affine_select(out=ident[:, :], in_=ident[:, :], compare_op=ALU.not_equal, fill=1.0, base=0,
                               pattern=[[-1, P]], channel_multiplier=1).then_inc(pool_const, 1)
            with pool.Fori(0, TURNS) as t:
                links = [0]

                def link(ins):
                    links[0] += 1
                    ins.then_inc(pool_link, 1)
                    pool.wait_ge(pool_link, t * POOL_LINKS + links[0])

                pool.wait_ge(stats1, (t + 1) * NB)
                link(pool.tensor_tensor(va[:, :], mv[:, :, 1], c_eps[:, :], ALU.add))
                pool.tensor_tensor(rs[:, :], va[:, :], c_mhalf[:, :], ALU.pow).then_inc(rstd1, 1)
                pool.wait_ge(cstats, (t + 1) * NB)
                link(pool.tensor_tensor(cva[:, :], cmv[:, :, 0], cmv[:, :, 0], ALU.mult))
                link(pool.tensor_tensor(cva[:, :], cva[:, :], cmv[:, :, 1], ALU.add))
                link(pool.tensor_tensor(cva[:, :], cva[:, :], c_eps[:, :], ALU.add))
                pool.tensor_tensor(crs[:, :], cva[:, :], c_mhalf[:, :], ALU.pow).then_inc(crstd, 1)

                def rotate(b):
                    for kq in range(2):
                        pool.wait_ge(d_read, t * D_USES + 3 * b + kq + 1)
                        pool.tensor_tensor(tc[:, b % 2, kq, :], tc[:, b % 2, kq, :], ts[:, kq, :], ALU.add).then_inc(rot_done, 1)

                def scale(kind, b, ready):
                    pool.wait_ge(ready, t * NB + b + 1)
                    n = kind * NB + b
                    for c in range(NC):
                        sl = prob[:, (n * NC + c) % E_SLOTS, :, :]
                        pool.tensor_tensor(sl, sl, coef[:, n % 2, c * HC:(c + 1) * HC].unsqueeze(2).broadcast_to([P, HC, P]),
                                           ALU.mult).then_inc(scaled[kind], 1)

                def invert(g):
                    pool.wait_ge(blk_in[g], 16 * (t + 1))
                    y = blk[:, g, :, :]
                    for k in range(1, Q - 1):
                        w = Q - 1 - k
                        o = outer[:, 0:k * w].rearrange("p (j i) -> p j i", j=k)
                        link(pool.tensor_tensor(o, y[:, 0:k, k:k + 1].broadcast_to([P, k, w]),
                                                y[:, k:k + 1, k + 1:Q].broadcast_to([P, k, w]), ALU.mult))
                        ins = pool.tensor_tensor(y[:, 0:k, k + 1:Q], y[:, 0:k, k + 1:Q], o, ALU.add)
                        if k < Q - 2:
                            link(ins)
                    ins.then_inc(pool_step, 1)
                    pool.wait_ge(pool_step, 5 + 2 * t + g + 1)
                    pool.nop().then_inc(passed["pool"], 1)
                    pool.memset(blk[:, g, :, :].rearrange("p j i -> p (j i)")[:, 0:Q * Q:Q + 1], 1.0).then_inc(inv_done, 1)

                rotate(0); rotate(1)
                for b in range(NB):
                    if b + 2 < NB:
                        rotate(b + 2)
                    scale(0, b, coef_low)
                invert(0); invert(1)
                pool.wait_ge(a_full, t * A_USES + a_att(NB - 1, NC - 1) + 1)
                pool.nop().then_inc(passed["pool"], 1)
                pool.memset(us[:, :, :], 0.0).then_inc(u_zero, 1)

                def cross_rstd(b):
                    pool.wait_ge(stats2, t * NB + b + 1)
                    link(pool.tensor_tensor(va[:, b:b + 1], mv[:, b, 1:2], c_1eps[:, b:b + 1], ALU.mult))
                    link(pool.tensor_tensor(va[:, b:b + 1], va[:, b:b + 1], c_eps2[:, b:b + 1], ALU.add))
                    pool.tensor_tensor(rs[:, b:b + 1], va[:, b:b + 1], c_mhalf[:, b:b + 1], ALU.pow).then_inc(rstd2, 1)

                def rotate_x(b):
                    pool.wait_ge(xq_prod, t * NB + b + 1)
                    if b >= 2:
                        pool.wait_ge(a_read, t * A_USES + a_xq(b - 2) + 1)
                    pool.tensor_tensor(tc[:, b % 2, 1, :].rearrange("p (c g d) -> p g c d", c=NC, g=G),
                                       tc[:, b % 2, 0, :].rearrange("p (g c d) -> p g c d", g=G, c=NC),
                                       ts[:, 0, :].rearrange("p (g c d) -> p g c d", g=G, c=NC), ALU.add).then_inc(xq_rot, 1)

                cross_rstd(0); cross_rstd(1); cross_rstd(2)
                rotate_x(0)
                cross_rstd(3)
                rotate_x(1)
                for b in range(NB):
                    if b + 2 < NB:
                        rotate_x(b + 2)
                    scale(2, b, coef_x)
                for b in range(NB):
                    pool.wait_ge(stats3, t * NB + b + 1)
                    link(pool.tensor_tensor(va[:, b:b + 1], mv[:, b, 1:2], c_eps[:, b:b + 1], ALU.add))
                    pool.tensor_tensor(rs[:, b:b + 1], va[:, b:b + 1], c_mhalf[:, b:b + 1], ALU.pow).then_inc(rstd3, 1)
                assert links[0] == POOL_LINKS, links
                pool.wait_ge(rstd3, (t + 1) * NB)
                pool.nop().then_inc(turn_done, 1)
                pool.wait_ge(turn_done, (t + 1) * 5)


_INS = ["x", "ctx_512", "L0_attn_Wq", "L0_attn_Wk", "L0_attn_Wv", "L0_attn_Wb", "L0_attn_bb", "L0_attn_Wo",
        "L0_xattn_q_norm_w", "L0_xattn_k_norm_w", "L0_xattn_w_out", "L0_ffn_Wr", "L0_ffn_br", "L0_ffn_Wd", "L0_ffn_bd",
        "L0_ffn_Wu", "L0_ffn_bu"]


def kernel(**inputs):
    import numpy as _np
    import concourse.bacc as _bacc
    from concourse import mybir as _mybir
    from concourse.bass_utils import run_bass_kernel_spmd as _run

    nc = _bacc.Bacc("TRN2", target_bir_lowering=False, num_devices=1)
    arrays, args = {}, []
    for name in _INS:
        a = _np.ascontiguousarray(inputs[name])
        arrays[f"in_{name}_dram"] = a
        args.append(nc.dram_tensor(f"in_{name}_dram", a.shape, _mybir.dt.from_np(a.dtype), kind="ExternalInput").ap())
    args.append(nc.dram_tensor("out_0_dram", inputs["x"].shape, _mybir.dt.float32, kind="ExternalOutput").ap())
    decoder_layer(nc, *args)
    r = _run(nc, [arrays], core_ids=[0])
    return r.results[0]["out_0_dram"]
```

```python
from contextlib import ExitStack

import numpy as np

import concourse.bass as bass
from concourse import mybir

F32 = mybir.dt.float32
BF16 = mybir.dt.bfloat16
ALU = mybir.AluOpType
ACT = mybir.ActivationFunctionType
AX = mybir.AxisListType

P = 128
D = 512
H = 16
DH = D // H
G = 4
CTX = G * DH
NC = D // P
HC = H // NC
NB = 4
Q = 32
NS = P // Q
E = 8
R = 16
EPS = 1e-5
THETA = 10000.0
BONUS = 3.0 * (1.0 - min(1 / 1250, 1.0))
NEG = -1e30
HH = H // 2

FIRST = {"a": 16, "d": 28, "s": 20, "dve": 72, "pool": 64}
BOTH = {"a": 77, "d": 50, "s": 48, "dve": 85, "pool": 139}


class Section:

    def __init__(self, name, start, turns, second, first):
        self.name, self.S, self.K = name, second is not None, first is not None
        self.gs, self.gk = second, first
        self.shift = 0 if self.S else 1
        self.base = {k: start[k] + turns * BOTH[k] for k in BOTH}


def first_section():
    return Section("first", {k: 0 for k in BOTH}, 0, None, 0)


def both_section(t):
    return Section("both", FIRST, t, t, t + 1)


def last_section(turns):
    return Section("last", FIRST, turns - 1, turns - 1, None)


def constants():
    tok = (np.arange(P)[:, None] - Q * np.arange(NB)[None, :]) % P
    half = DH // 2
    inv = (1.0 / np.float32(THETA) ** (np.arange(half, dtype=np.float32) / np.float32(half))).astype(np.float32)
    ang = tok.astype(np.float32)[:, :, None] * inv
    root = np.float32(DH ** -0.25)
    cos, sin = np.cos(ang) * root, np.sin(ang) * root
    rope = np.stack([np.concatenate([cos, cos], -1), np.concatenate([-sin, sin], -1)], 2)
    earlier = tok[:, :, None] > tok.T[None, :, :]
    upto = tok[:, :, None] >= tok.T[None, :, :]
    mask = np.stack([np.where(earlier, 0.0, NEG), np.where(upto, 0.0, NEG)], 1)
    notfirst = np.where(tok == 0, 0.0, -1.0)
    before = np.tile((np.arange(E)[None, :] < np.arange(E)[:, None]).astype(np.float32)[None], (P, 1, 1))
    return (rope.astype(np.float32), mask.astype(np.float32), notfirst.astype(np.float32), before)


def pieces(b):
    if b == 0:
        return [(0, 0, P)]
    return [(0, Q * b, P - Q * b), (P - Q * b, 0, Q * b)]


def decoder_layer(nc, x, ctx_512, Wq, Wk, Wv, Wb, bb, Wo, qnw, knw, w_out, Wr, br, Wd, bd, Wu, bu, out):
    B = x.shape[0]
    TURNS = B // NB
    rope_c, mask_c, notfirst_c, before_c = constants()
    rope_d = nc.inline_tensor(rope_c, name="rope_c").ap()
    mask_d = nc.inline_tensor(mask_c, name="mask_c").ap()
    notfirst_d = nc.inline_tensor(notfirst_c, name="notfirst_c").ap()
    before_d = nc.inline_tensor(before_c, name="before_c").ap()
    blk_d = nc.dram_tensor("blk_d", [NB, H, NS, Q, Q], F32).ap()
    inv_d = nc.dram_tensor("inv_d", [NB, H, NS, Q, Q], F32).ap()

    with ExitStack() as stack:
        def sb(name, shape, dt=F32):
            return stack.enter_context(nc.sbuf_tensor(name, shape, dt))

        def sem(name):
            return stack.enter_context(nc.semaphore(name))

        wq = sb("wq", [P, NC, D]); wk = sb("wk", [P, NC, D]); wv = sb("wv", [P, NC, D])
        wb = sb("wb", [P, NC, H]); wo = sb("wo", [P, NC, D]); woutT = sb("woutT", [P, NC, D])
        wdr = sb("wdr", [P, NC, E * R + E]); wu = sb("wu", [P, D]); bu_s = sb("bu_s", [P, D])
        bb_s = sb("bb_s", [P, H]); qnw_s = sb("qnw_s", [P, D]); knw_s = sb("knw_s", [P, CTX])
        brb = sb("brb", [P, E]); bd_s = sb("bd_s", [P, E * R])
        rope = sb("rope", [P, NB, 2, DH]); masks = sb("masks", [P, 2, NB, P], BF16)
        notfirst = sb("notfirst", [P, NB]); before = sb("before", [P, E, E])
        ident = sb("ident", [P, P]); identb = sb("identb", [P, P], BF16)
        c_eps = sb("c_eps", [P, NB]); c_mhalf = sb("c_mhalf", [P, NB])
        c_1eps = sb("c_1eps", [P, NB]); c_eps2 = sb("c_eps2", [P, NB])

        st6 = sb("st6", [P, NB, 6]); mv = sb("mv", [P, NB, 2]); va = sb("va", [P, NB]); rs = sb("rs", [P, NB])
        ct6 = sb("ct6", [P, NB, 6]); cmv = sb("cmv", [P, NB, 2]); cva = sb("cva", [P, NB]); crs = sb("crs", [P, NB])
        xt6 = sb("xt6", [P, NB, 6]); xmv = sb("xmv", [P, NB, 2]); xva = sb("xva", [P, NB]); xrs = sb("xrs", [P, NB])
        xn = sb("xn", [P, 2, D])
        hT = sb("hT", [P, 2, NC, P])
        tc = sb("tc", [P, 2, D]); ts = sb("ts", [P, 2, D])
        kT = sb("kT", [P, NB, NC, P]); qT = sb("qT", [P, NB, NC, P])
        kbd = sb("kbd", [P, 2, NC, HC, P])
        beta = sb("beta", [P, NB, H])
        vst = sb("vst", [P, NS, D])
        lowT = sb("lowT", [P, NB, H, P])
        blk = sb("blk", [P, 2, Q, Q])
        outer = sb("outer", [P, (Q // 2) ** 2])
        nmax = sb("nmax", [P, 2, H]); den = sb("den", [P, 2, H]); coef = sb("coef", [P, 2, H])
        prob = sb("prob", [P, 2, NC, HC, P])
        outer2 = tc[:, 0, 0:(Q // 2) ** 2]
        us = blk[:, :, :, :].rearrange("p a j i -> p (a j i)").rearrange("p (b n) -> p b n", b=NB)
        attT = sb("attT", [P, H, P])
        oT = sb("oT", [P, 2, NC, P])
        xs = sb("xs", [P, NB, D]); ctx = sb("ctx", [P, NB, CTX])
        xa = sb("xa", [P, 2, D])
        tmp = xa[:, 0, :].rearrange("p (a n) -> p a n", a=2)
        xr = sb("xr", [P, D])
        ckr = xr[:, :].rearrange("p (b n) -> p b n", b=NB)
        cks = xa[:, 1, :].rearrange("p (b n) -> p b n", b=NB)
        queries = [xr[:, :], xr[:, :], tc[:, 0, :], tc[:, 1, :]]
        h1 = xr[:, :].rearrange("p (b n) -> p b n", b=NB)
        qxT = sb("qxT", [P, NC, P])
        inv23 = [xa[:, 1, :].rearrange("p (h i) -> p h i", h=H), qxT[:, :, :].rearrange("p c j -> p (c j)").rearrange("p (h i) -> p h i", h=H)]
        kxbd = sb("kxbd", [P, NB, G, P])
        gates = sb("gates", [P, (NB - 1) * E + P])
        hwT = oT[:, :, 0:2, :].rearrange("p a c j -> p a (c j)")
        cmp1 = ts[:, 0, 0:2 * E * E].rearrange("p (b e f) -> p b e f", b=2, e=E)
        cmp2 = ts[:, 1, 0:2 * E * E].rearrange("p (b e f) -> p b e f", b=2, e=E)
        lg = sb("lg", [P, NB, E]); lmax = sb("lmax", [P, NB]); ex = sb("ex", [P, NB, E])
        rank = sb("rank", [P, NB, E]); wsel = sb("wsel", [P, NB, E]); wsum = sb("wsum", [P, NB])

        bank = [stack.enter_context(nc.psum_tensor(f"bank{i}", [P, 512], F32)) for i in range(8)]
        ring_a, ring_d, ring_s = bank[0:3], bank[3:5], bank[5:8]
        a_full = sem("a_full"); a_read = sem("a_read"); d_full = sem("d_full"); d_read = sem("d_read")
        s_full = sem("s_full"); max_ready = sem("max_ready"); exp_done = sem("exp_done")
        loaded = sem("loaded"); loaded_k = sem("loaded_k"); mask_in = sem("mask_in"); table_done = sem("table_done"); pool_const = sem("pool_const")
        bu_zero = sem("bu_zero"); pool_step = sem("pool_step"); wout_full = sem("wout_full"); wout_done = sem("wout_done")
        x_in = [sem(f"x_in{b}") for b in range(NB)]; r_in = [sem(f"r_in{b}") for b in range(NB)]
        c_in = [sem(f"c_in{b}") for b in range(NB)]
        stats1 = sem("stats1"); rstd1 = sem("rstd1"); norm1 = sem("norm1"); rope_prod = sem("rope_prod"); rot_done = sem("rot_done")
        cstats = sem("cstats"); crstd = sem("crstd"); ck_rot = sem("ck_rot")
        stats2 = sem("stats2"); rstd2 = sem("rstd2"); xq_prod = sem("xq_prod"); xq_rot = sem("xq_rot")
        stats3 = sem("stats3"); rstd3 = sem("rstd3"); norm3 = sem("norm3")
        coef_low = sem("coef_low")
        scaled = {"low": sem("scaled_low"), "att": sem("scaled_att"), "x": sem("scaled_x")}
        kbd_in = [sem("kbd_in0"), sem("kbd_in1")]
        blk_out = [sem(f"blk_out{b}") for b in range(NB)]; blk_in = [sem("blk_in0"), sem("blk_in1")]
        inv_done = [sem("inv_done0"), sem("inv_done1")]; inv_out = [sem("inv_out0"), sem("inv_out1")]; inv_in = [sem("inv_in0"), sem("inv_in1")]
        u_zero = sem("u_zero"); tmp_ready = sem("tmp_ready")
        gate_max = sem("gate_max"); gate_exp = sem("gate_exp"); hw_ready = sem("hw_ready")
        dve_link = sem("dve_link"); pool_link = sem("pool_link"); stored = sem("stored")
        passed = {e: sem(f"passed_{e}") for e in ("sp", "pe", "dve", "pool")}
        N_LOADS, N_LOADS_K = 29, 7

        block = stack.enter_context(nc.Block())

        place = {(n, r): {} for n in ("first", "both", "last") for r in "ads"}

        def after(sec, ring, what):
            return sec.base[ring] + place[sec.name, ring][what] + 1

        def half(sec, kind, b):
            return 1 if (kind, b) == ("att", 0) else (place[sec.name, "s"][kind, b, 0] // NC + sec.shift) % 2

        def heads(ap):
            return ap.rearrange("p (h d) -> p h d", d=DH)

        def flat(ap):
            return ap.rearrange("p c j -> p (c j)")

        @block.tensor
        def _(pe):
            def transpose_wout():
                pe.wait_ge(loaded, 16 * N_LOADS)
                pe.wait_ge(a_read, FIRST["a"])
                for c in range(NC):
                    if c >= 2:
                        pe.wait_ge(wout_done, c - 1)
                    for o in range(NC):
                        mm = pe.transpose(ring_a[c % 2][:, o * P:(o + 1) * P], attT[:, o * NC + c, :], ident[:, :])
                    mm.then_inc(wout_full, 1)
                pe.wait_ge(wout_done, NC)

            def section(sec):
                S, K, gs, gk = sec.S, sec.K, sec.gs, sec.gk

                def fill(ring, banks, read, what, needs=None):
                    at = place[sec.name, ring]
                    n = at[what] = len(at)
                    taken = n - len(banks) + 1
                    if needs:
                        taken = max(taken, at[needs] + 1)
                    if taken > 0:
                        pe.wait_ge(read, sec.base[ring] + taken)
                    elif S:
                        pe.wait_ge(read, sec.base[ring])
                    return banks[n % len(banks)]

                def fill_a(*what, needs=None):
                    return fill("a", ring_a, a_read, what, needs)

                def fill_d(*what):
                    return fill("d", ring_d, d_read, what)

                def rows_T(src, *what):
                    ps = fill_a(*what)
                    for c in range(NC):
                        mm = pe.transpose(ps[:, c * P:(c + 1) * P], src(c), ident[:, :])
                    mm.then_inc(a_full, 1)

                def norm_T(b):
                    pe.wait_ge(norm1, gk * NB + b + 1)
                    rows_T(lambda c: xn[:, b % 2, c * P:(c + 1) * P], "norm", b)

                def project(b, name):
                    w = {"v": wv, "k": wk, "q": wq, "beta": wb}[name]
                    if name == "k":
                        pe.wait_ge(a_read, after(sec, "a", ("norm", b)))
                    ps = fill_a("v", b) if name == "v" else fill_d(name, b)
                    n = w.shape[2]
                    for c in range(NC):
                        mm = pe.matmul(ps[:, 0:n], hT[:, b % 2, c, :], w[:, c, :], start=(c == 0), stop=(c == NC - 1))
                    mm.then_inc(a_full if name == "v" else d_full, 1)

                def rotated_T(b):
                    for kq in range(2):
                        pe.wait_ge(rot_done, gk * 2 * NB + 2 * b + kq + 1)
                        rows_T(lambda c: tc[:, kq, c * P:(c + 1) * P], "kT" if kq == 0 else "qT", b)

                def scores(stat, keys, mask, kind, b, chunks=range(NC)):
                    for c in chunks:
                        ps = fill("s", ring_s, exp_done, (kind, b, c))
                        pe.matmul(ps[:, :], stat(c), keys(c), start=True, stop=False)
                        pe.matmul(ps[:, :].rearrange("p (h j) -> p h j", h=HC), identb[:, :],
                                  masks[:, mask, b, :].unsqueeze(1).broadcast_to([P, HC, P]),
                                  start=False, stop=True).then_inc(s_full, 1)

                def key_scores(b, chunks=range(NC)):
                    pe.wait_ge(kbd_in[b % 2], 16 * HC * (gk * 4 + b // 2 + 1))
                    scores(lambda c: kT[:, b, c, :], lambda c: kbd[:, b % 2, c, :, :], 0, "low", b, chunks)

                def query_scores(b, g, chunks):
                    pe.wait_ge(kbd_in[b % 2], 16 * HC * (g * 4 + 2 + b // 2 + 1))
                    scores(lambda c: qT[:, b, c, :], lambda c: kbd[:, b % 2, c, :, :], 1, "att", b, chunks)

                def probs_T(kind, b, g, chunks=range(NC)):
                    for c in chunks:
                        pe.wait_ge(scaled[kind], g * NB * NC + b * NC + c + 1)
                        ps = fill_d(kind, b, c) if kind == "low" else fill_a(kind, b, c)
                        for r in range(HC):
                            mm = pe.transpose(ps[:, r * P:(r + 1) * P], prob[:, half(sec, kind, b), c, r, :], ident[:, :])
                        mm.then_inc(d_full if kind == "low" else a_full, 1)

                def solve_rhs(s):
                    for f in range(2):
                        pe.wait_ge(a_read, after(sec, "a", ("u", s - 1, f)))
                        ps = fill_d("rhs", s, f)
                        for h in range(f * HH, f * HH + HH):
                            for b in range(NB):
                                q = Q * ((s + b) % NS)
                                mm = pe.matmul(ps[q:q + Q, (h % HH) * DH:(h % HH + 1) * DH], lowT[:, b, h, q:q + Q],
                                               us[:, b, h * DH:(h + 1) * DH], start=True, stop=True)
                        mm.then_inc(d_full, 1)

                def inverse(b, h, q):
                    return lowT[q:q + Q, b, h, q:q + Q] if b < 2 else inv23[b - 2][q:q + Q, h, :]

                def solve_blocks(s):
                    for f in range(2):
                        if s > 0:
                            pe.wait_ge(tmp_ready, gs * 2 * (NS - 1) + 2 * (s - 1) + f + 1)
                        ps = fill_a("u", s, f)
                        pe.nop().then_inc(passed["pe"], 1)
                        for h in range(f * HH, f * HH + HH):
                            for b in range(NB):
                                q = Q * ((s + b) % NS)
                                rhs = tmp[q:q + Q, f, (h % HH) * DH:(h % HH + 1) * DH] if s > 0 else vst[q:q + Q, 0, h * DH:(h + 1) * DH]
                                mm = pe.matmul(ps[q:q + Q, (h % HH) * DH:(h % HH + 1) * DH], inverse(b, h, q), rhs, start=True, stop=True)
                        mm.then_inc(a_full, 1)

                def mix(vals, b, *what, needs=None):
                    ps = fill_a(*what, needs=needs)
                    for c in range(NC):
                        for r in range(HC):
                            mm = pe.matmul(ps[Q * r:Q * r + Q, c * P:(c + 1) * P], vals(c, r), attT[:, c * HC + r, :], start=True, stop=True)
                    mm.then_inc(a_full, 1)

                def att_mix(b):
                    mix(lambda c, r: us[:, b, (c * HC + r) * DH:(c * HC + r + 1) * DH], b, "mix", b,
                        needs=("att", b, NC - 1) if b >= 1 else ("u", NS - 1, 1))

                def out_proj(w, place_a, b, *what):
                    pe.wait_ge(a_read, after(sec, "a", place_a))
                    ps = fill_d(*what)
                    for c in range(NC):
                        mm = pe.matmul(ps[:, :], oT[:, b % 2, c, :], w[:, c, :], start=(c == 0), stop=(c == NC - 1))
                    mm.then_inc(d_full, 1)

                def att_out(b):
                    out_proj(wo, ("mix", b), b, "out", b)

                def context_T():
                    pe.wait_ge(ck_rot, gs + 1)
                    rows_T(lambda b: ckr[:, b, :], "ck")

                def xq_T(b):
                    pe.wait_ge(xq_rot, gs * NB + b + 1)
                    rows_T(lambda c: queries[b][:, c * P:(c + 1) * P], "xq", b)

                def cross_scores(b, chunks):
                    pe.wait_ge(a_read, after(sec, "a", ("xq", b)))
                    scores(lambda c: qxT[:, c, :], lambda c: kxbd[:, b, :, :], 1, "x", b, chunks)

                def cross_mix(b):
                    mix(lambda c, r: ctx[:, b, r * DH:(r + 1) * DH], b, "xmix", b, needs=("x", b, NC - 1))

                def cross_out(b):
                    out_proj(woutT, ("xmix", b), b, "xout", b)

                def norm3_T(b):
                    pe.wait_ge(norm3, gs * NB + b + 1)
                    rows_T(lambda c: xa[:, b % 2, c * P:(c + 1) * P], "norm3", b)

                def hidden(b):
                    pe.wait_ge(a_read, after(sec, "a", ("norm3", b)))
                    ps = fill_d("hid", b)
                    for c in range(NC):
                        mm = pe.matmul(ps[:, 0:E * R + E], hT[:, b % 2, c, :], wdr[:, c, :], start=(c == 0), stop=(c == NC - 1))
                    mm.then_inc(d_full, 1)

                def gated_T(b):
                    pe.wait_ge(hw_ready, gs * NB + b + 1)
                    ps = fill_a("hw", b)
                    pe.transpose(ps[:, 0:P], h1[:, b, :], ident[:, :])
                    pe.transpose(ps[:, P:2 * P], gates[:, b * E:b * E + P], ident[:, :]).then_inc(a_full, 1)

                def up(b):
                    pe.wait_ge(a_read, after(sec, "a", ("hw", b)))
                    ps = fill_d("ffn", b)
                    pe.matmul(ps[:, :], hwT[:, b % 2, 0:P], wu[:, :], start=True, stop=False)
                    pe.matmul(ps[:, :], hwT[:, b % 2, P:2 * P], bu_s[:, :], start=False, stop=True).then_inc(d_full, 1)

                def cross_step(b, rest=range(2, NC)):
                    probs_T("x", b, gs, lo); cross_scores(b + 1, [0]); probs_T("x", b, gs, hi); cross_scores(b + 1, [1])
                    cross_mix(b); cross_scores(b + 1, rest)

                lo, hi = range(0, 2), range(2, NC)
                if S:
                    probs_T("att", 0, gs)
                if K:
                    norm_T(0); project(0, "k")
                if S:
                    for g in range(2):
                        pe.wait_ge(inv_in[g], 16 * (2 * NS, 2)[g] * (gs + 1))
                    solve_blocks(0); query_scores(1, gs, [0]); solve_rhs(1); query_scores(1, gs, [1])
                    solve_blocks(1); query_scores(1, gs, [2]); solve_rhs(2); query_scores(1, gs, [3]); solve_blocks(2)
                if K:
                    norm_T(1)
                if S:
                    solve_rhs(3)
                if K:
                    project(0, "q")
                if S:
                    solve_blocks(3)
                if K:
                    project(0, "v"); project(0, "beta")
                if S:
                    att_mix(0); probs_T("att", 1, gs); att_out(0); query_scores(2, gs, lo)
                if K:
                    rotated_T(0)
                if S:
                    query_scores(2, gs, hi); att_mix(1)
                if K:
                    project(1, "k")
                if S:
                    probs_T("att", 2, gs); att_out(1); query_scores(3, gs, lo)
                if K:
                    project(1, "q")
                if S:
                    query_scores(3, gs, hi)
                if K:
                    project(1, "v"); project(1, "beta")
                if S:
                    att_mix(2)
                if K:
                    rotated_T(1); norm_T(2)
                if S:
                    probs_T("att", 3, gs); att_out(2)
                if K:
                    key_scores(0, lo); project(2, "k"); key_scores(0, hi); project(2, "q")
                if S:
                    context_T(); att_mix(3)
                if K:
                    project(2, "v"); project(2, "beta")
                if S:
                    att_out(3)
                if K:
                    rotated_T(2); norm_T(3); probs_T("low", 0, gk, lo); key_scores(1, lo); probs_T("low", 0, gk, hi)
                    project(3, "k"); key_scores(1, hi)
                if S:
                    xq_T(0)
                if K:
                    project(3, "q")
                if S:
                    cross_scores(0, lo)
                if K:
                    project(3, "v"); project(3, "beta")
                if K:
                    probs_T("low", 1, gk, lo)
                if S:
                    cross_scores(0, [2])
                if K:
                    probs_T("low", 1, gk, hi)
                if S:
                    cross_scores(0, [3])
                if K:
                    rotated_T(3); key_scores(2, lo)
                if S:
                    xq_T(1)
                if K:
                    key_scores(2, hi)
                if S:
                    cross_step(0); cross_out(0)
                if K:
                    probs_T("low", 2, gk, lo); key_scores(3, [0]); probs_T("low", 2, gk, hi)
                if S:
                    xq_T(2)
                if K:
                    key_scores(3, [1, 2, 3])
                if S:
                    cross_step(1, [])
                if K:
                    probs_T("low", 3, gk, lo)
                if S:
                    cross_scores(2, [2])
                if K:
                    probs_T("low", 3, gk, hi)
                if S:
                    cross_scores(2, [3]); cross_out(1)
                    xq_T(3); probs_T("x", 2, gs, lo); cross_scores(3, [0]); probs_T("x", 2, gs, hi); cross_scores(3, [1])
                    cross_mix(2); cross_scores(3, [2]); norm3_T(0); cross_scores(3, [3]); cross_out(2); hidden(0)
                if K:
                    query_scores(0, gk, lo)
                if S:
                    probs_T("x", 3, gs, lo)
                if K:
                    query_scores(0, gk, [2])
                if S:
                    probs_T("x", 3, gs, hi); cross_mix(3); norm3_T(1); norm3_T(2); cross_out(3); hidden(1); hidden(2)
                if K:
                    query_scores(0, gk, [3])
                if S:
                    norm3_T(3); gated_T(0); hidden(3); gated_T(1); up(0); up(1); gated_T(2); gated_T(3); up(2); up(3)
                if sec.name != "last":
                    used = {r: len(place[sec.name, r]) for r in "ads"}
                    want = FIRST if sec.name == "first" else BOTH
                    assert all(used[r] == want[r] for r in "ads"), used

            pe.wait_ge(pool_const, 1)
            pe.wait_ge(table_done, 3)
            pe.wait_ge(loaded_k, 16 * N_LOADS_K)
            section(first_section())
            transpose_wout()
            with pe.Fori(0, TURNS - 1) as t:
                section(both_section(t))
            section(last_section(TURNS))

        @block.scalar
        def _(act):
            def section(sec):
                S, K, gs, gk = sec.S, sec.K, sec.gs, sec.gk
                read = []

                def from_a(*what):
                    assert place[sec.name, "a"][what] == len(read), (what, place[sec.name, "a"][what], len(read))
                    read.append(what)
                    act.wait_ge(a_full, after(sec, "a", what))
                    return ring_a[(len(read) - 1) % 3]

                def copy_out(dst, *what, cols=512):
                    act.activation(dst, from_a(*what)[:, 0:cols], ACT.Copy).then_inc(a_read, 1)

                def norm_out(b):
                    if b >= 2:
                        act.wait_ge(d_full, after(sec, "d", ("beta", b - 2)))
                    copy_out(flat(hT[:, b % 2, :, :]), "norm", b)

                def values_out(b):
                    ps = from_a("v", b)
                    for s in range(NS):
                        q = Q * ((s + b) % NS)
                        ins = act.activation(vst[q:q + Q, s, :], ps[q:q + Q, :], ACT.Copy)
                    ins.then_inc(a_read, 1)

                def rotated_out(b):
                    copy_out(flat(kT[:, b, :, :]), "kT", b)
                    copy_out(flat(qT[:, b, :, :]), "qT", b)

                def exps(kind, b, chunks=range(NC)):
                    for c in chunks:
                        i = place[sec.name, "s"][kind, b, c]
                        n = i // NC
                        act.wait_ge(max_ready, after(sec, "s", (kind, b, c)))
                        if n >= 2:
                            last = [w for w, at in place[sec.name, "s"].items() if at == i - 2 * NC][0]
                            if last[0] == "low":
                                act.wait_ge(d_full, after(sec, "d", last))
                            else:
                                act.wait_ge(a_full, after(sec, "a", last))
                        for r in range(HC):
                            h = c * HC + r
                            ins = act.activation(prob[:, half(sec, kind, b), c, r, :], ring_s[i % 3][:, r * P:(r + 1) * P], ACT.Exp,
                                                 bias=nmax[:, half(sec, kind, b), h:h + 1], accum_out=den[:, half(sec, kind, b), h:h + 1])
                        ins.then_inc(exp_done, 1)

                def solved(s):
                    for f in range(2):
                        ps = from_a("u", s, f)
                        for b in range(NB):
                            q = Q * ((s + b) % NS)
                            ins = act.activation(us[q:q + Q, b, f * HH * DH:(f + 1) * HH * DH], ps[q:q + Q, 0:HH * DH], ACT.Copy)
                        ins.then_inc(a_read, 1)

                def att_T_out(b, kind="att", chunks=range(NC)):
                    for c in chunks:
                        copy_out(flat(attT[:, c * HC:(c + 1) * HC, :]), kind, b, c)

                def mix_out(kind, b):
                    if b >= 2:
                        act.wait_ge(d_full, after(sec, "d", ("out" if kind == "mix" else "xout", b - 2)))
                    elif kind == "xmix":
                        act.wait_ge(d_full, after(sec, "d", ("out", b + 2)))
                    copy_out(flat(oT[:, b % 2, :, :]), kind, b)

                def xq_out(b):
                    copy_out(flat(qxT[:, :, :]), "xq", b)

                def norm3_out(b):
                    if b >= 2:
                        act.wait_ge(d_full, after(sec, "d", ("hid", b - 2)))
                    elif K:
                        act.wait_ge(d_full, after(sec, "d", ("beta", b + 2)))
                    copy_out(flat(hT[:, b % 2, :, :]), "norm3", b)

                def gate_exps(a):
                    act.wait_ge(gate_max, gs * 2 + a + 1)
                    act.activation(ex[:, 2 * a:2 * a + 2, :], lg[:, 2 * a:2 * a + 2, :], ACT.Exp).then_inc(gate_exp, 1)

                def gated_out(b):
                    if b >= 2:
                        act.wait_ge(d_full, after(sec, "d", ("ffn", b - 2)))
                    copy_out(hwT[:, b % 2, :], "hw", b, cols=2 * P)

                def context_out():
                    ps = from_a("ck")
                    for g in range(G):
                        ins = act.activation(kxbd[Q * g:Q * g + Q, :, g, :],
                                             ps[Q * g:Q * g + Q, :].rearrange("p (b j) -> p b j", b=NB), ACT.Copy)
                    ins.then_inc(a_read, 1)

                lo, hi = range(0, 2), range(2, NC)
                if S and K:
                    for b in (0, 1):
                        for t0, p0, n in pieces(b):
                            act.dma_start(xn[p0:p0 + n, b, :],
                                          x[bass.ds(gk * NB + b, 1), t0:t0 + n, :].rearrange("o t d -> (o t) d")).then_inc(x_in[b], 16)
                if S:
                    act.wait_ge(d_full, sec.base["d"])
                    att_T_out(0)
                if K:
                    norm_out(0)
                if S:
                    act.wait_ge(u_zero, gs + 1)
                    solved(0); exps("att", 1, [0]); solved(1); exps("att", 1, [1, 2]); solved(2); exps("att", 1, [3])
                if K:
                    norm_out(1)
                if S:
                    solved(3)
                if K:
                    values_out(0)
                if S:
                    mix_out("mix", 0); att_T_out(1); exps("att", 2, lo)
                if K:
                    rotated_out(0)
                if S:
                    exps("att", 2, hi); mix_out("mix", 1); att_T_out(2); exps("att", 3)
                if K:
                    values_out(1)
                if S:
                    mix_out("mix", 2)
                if K:
                    rotated_out(1); norm_out(2)
                if S:
                    att_T_out(3)
                if K:
                    exps("low", 0)
                if S:
                    context_out(); mix_out("mix", 3)
                if K:
                    values_out(2); rotated_out(2); norm_out(3); exps("low", 1)
                if S:
                    xq_out(0); exps("x", 0, lo)
                if K:
                    values_out(3)
                if S:
                    exps("x", 0, hi)
                if K:
                    rotated_out(3); exps("low", 2, lo)
                if S:
                    xq_out(1)
                if K:
                    exps("low", 2, hi)
                if S:
                    att_T_out(0, "x"); exps("x", 1, [0]); mix_out("xmix", 0); exps("x", 1, range(1, NC))
                if K:
                    exps("low", 3, [0])
                if S:
                    xq_out(2)
                if K:
                    exps("low", 3, [1, 2, 3])
                if S:
                    att_T_out(1, "x"); exps("x", 2, [0]); mix_out("xmix", 1); exps("x", 2, range(1, NC))
                    xq_out(3); att_T_out(2, "x"); exps("x", 3, [0]); mix_out("xmix", 2); norm3_out(0); exps("x", 3, range(1, NC))
                if K:
                    exps("att", 0, [0])
                if S:
                    att_T_out(3, "x", lo)
                    att_T_out(3, "x", hi)
                if K:
                    exps("att", 0, [1])
                if S:
                    mix_out("xmix", 3); norm3_out(1); norm3_out(2)
                if K:
                    exps("att", 0, [2])
                if S:
                    gate_exps(0); norm3_out(3)
                if K:
                    exps("att", 0, [3])
                if S:
                    gated_out(0); gated_out(1); gate_exps(1); gated_out(2); gated_out(3)

            section(first_section())
            for c in range(NC):
                act.wait_ge(wout_full, c + 1)
                act.activation(woutT[:, c, :], ring_a[c % 2][:, :], ACT.Copy).then_inc(wout_done, 1)
            with act.Fori(0, TURNS - 1) as t:
                section(both_section(t))
            section(last_section(TURNS))

        @block.vector
        def _(dve):
            dve.memset(bu_s[:, :], 0.0).then_inc(bu_zero, 1)
            dve.memset(kbd[:, :, :, :, :], 0.0).then_inc(table_done, 1)
            dve.memset(kxbd[:, :, :, :], 0.0)
            dve.memset(gates[:, :], 0.0)
            dve.wait_ge(mask_in, 16)
            dve.tensor_copy(masks[:, :, :, :].rearrange("p a b j -> p (a b) j"), lowT[:, 0, 0:2 * NB, :]).then_inc(table_done, 1)
            dve.wait_ge(pool_const, 1)
            dve.tensor_copy(identb[:, :], ident[:, :]).then_inc(table_done, 1)
            dve.wait_ge(loaded_k, 16 * N_LOADS_K)
            dve.wait_ge(table_done, 3)

            def swapped(ap):
                return ap.rearrange("p (h a d) -> p h a d", a=2, d=DH // 2)[:, :, ::-1, :]

            def halves(ap):
                return ap.rearrange("p (h a d) -> p h a d", a=2, d=DH // 2)

            def table(b, k, n):
                return rope[:, b, k, :].unsqueeze(1).broadcast_to([P, n, DH])

            def table2(b, k, n):
                return rope[:, b, k, :].rearrange("p (a d) -> p a d", a=2).unsqueeze(1).broadcast_to([P, n, 2, DH // 2])

            def section(sec):
                S, K, gs, gk = sec.S, sec.K, sec.gs, sec.gk
                links, read = [0], []

                def link(ins):
                    links[0] += 1
                    ins.then_inc(dve_link, 1)
                    dve.wait_ge(dve_link, sec.base["dve"] + links[0])

                def from_d(*what):
                    assert place[sec.name, "d"][what] == len(read), (what, place[sec.name, "d"][what], len(read))
                    read.append(what)
                    dve.wait_ge(d_full, after(sec, "d", what))
                    return ring_d[(len(read) - 1) % 2]

                def stats(rows, s6, m, done):
                    link(dve.bn_stats(s6, rows))
                    dve.nop().then_inc(passed["dve"], 1)
                    dve.bn_aggr(m, s6).then_inc(done, 1)

                def row_stats(b):
                    dve.wait_ge(x_in[b], 16 * len(pieces(b)) * (gk + 1))
                    stats(xn[:, b % 2, :], st6[:, b, :], mv[:, b, :], stats1)

                def norm(b):
                    dve.wait_ge(rstd1, gk * NB + b + 1)
                    dve.tensor_scalar(xn[:, b % 2, :], xn[:, b % 2, :], mv[:, b, 0:1], rs[:, b:b + 1],
                                      ALU.subtract, ALU.mult).then_inc(norm1, 1)

                def context_stats():
                    for b in range(NB):
                        dve.wait_ge(c_in[b], 16 * len(pieces(b)) * (gs + 1))
                        stats(ctx[:, b, :], ct6[:, b, :], cmv[:, b, :], cstats)

                def context_keys():
                    dve.wait_ge(crstd, gs + 1)
                    for b in range(NB):
                        ins = dve.scalar_tensor_tensor(ckr[:, b, :], ctx[:, b, :], crs[:, b:b + 1], knw_s[:, :], ALU.mult, ALU.mult)
                    link(ins)
                    for b in range(NB):
                        ins = dve.tensor_tensor(halves(cks[:, b, :]), swapped(ckr[:, b, :]), table2(b, 1, G), ALU.mult)
                    link(ins)
                    for b in range(NB):
                        ins = dve.tensor_tensor(heads(ckr[:, b, :]), heads(ckr[:, b, :]), table(b, 0, G), ALU.mult)
                    link(ins)
                    dve.tensor_tensor(ckr[:, :, :], ckr[:, :, :], cks[:, :, :], ALU.add).then_inc(ck_rot, 1)

                def rope_products(b, name):
                    kq = 0 if name == "k" else 1
                    if b >= 1:
                        dve.wait_ge(a_full, after(sec, "a", (name + "T", b - 1)))
                    ps = from_d(name, b)
                    dve.tensor_tensor(heads(tc[:, kq, :]), heads(ps[:, :]), table(b, 0, H), ALU.mult)
                    dve.tensor_tensor(halves(ts[:, kq, :]), swapped(ps[:, :]), table2(b, 1, H), ALU.mult).then_inc(d_read, 1)

                def beta_out(b):
                    ps = from_d("beta", b)
                    dve.tensor_tensor(beta[:, b, :], ps[:, 0:H], bb_s[:, :], ALU.add).then_inc(d_read, 1)

                def row_max(kind, b, chunks=range(NC)):
                    for c in chunks:
                        i = place[sec.name, "s"][kind, b, c]
                        n = i // NC
                        dve.wait_ge(s_full, after(sec, "s", (kind, b, c)))
                        if n >= 2:
                            dve.wait_ge(exp_done, sec.base["s"] + i - 2 * NC + 1)
                        dve.tensor_reduce(nmax[:, half(sec, kind, b), c * HC:(c + 1) * HC], ring_s[i % 3][:, :].rearrange("p (h j) -> p h j", h=HC),
                                          AX.X, ALU.max, negate=True).then_inc(max_ready, 1)

                def low_factors(b):
                    a = half(sec, "low", b)
                    dve.wait_ge(exp_done, after(sec, "s", ("low", b, NC - 1)))
                    if b >= 1:
                        dve.wait_ge(scaled["low"], gk * NB * NC + b * NC)
                    link(dve.reciprocal(coef[:, a, :], den[:, a, :]))
                    dve.scalar_tensor_tensor(coef[:, a, :], coef[:, a, :], notfirst[:, b:b + 1], beta[:, b, :],
                                             ALU.mult, ALU.mult).then_inc(coef_low, 1)

                def scale_low(b, chunks):
                    a = half(sec, "low", b)
                    dve.wait_ge(coef_low, gk * NB + b + 1)
                    for c in chunks:
                        sl = prob[:, a, c, :, :]
                        dve.tensor_tensor(sl, sl, coef[:, a, c * HC:(c + 1) * HC].unsqueeze(2).broadcast_to([P, HC, P]),
                                          ALU.mult).then_inc(scaled["low"], 1)

                def low_out(b, chunks=range(NC)):
                    for c in chunks:
                        ps = from_d("low", b, c)
                        dve.tensor_copy(flat(lowT[:, b, c * HC:(c + 1) * HC, :]), ps[:, :]).then_inc(d_read, 1)

                def scale(kind, b, chunks=range(NC)):
                    a = half(sec, kind, b)
                    if 0 in chunks and ((K and kind == "x" and b == NB - 1) or (kind == "att" and b == 1)):
                        dve.wait_ge(scaled["low"], ((gk if kind == "x" else gs) + 1) * NB * NC)
                    for c in chunks:
                        r, sl = coef[:, a, c * HC:(c + 1) * HC], prob[:, a, c, :, :]
                        dve.wait_ge(exp_done, after(sec, "s", (kind, b, c)))
                        link(dve.reciprocal(r, den[:, a, c * HC:(c + 1) * HC]))
                        dve.tensor_tensor(sl, sl, r.unsqueeze(2).broadcast_to([P, HC, P]), ALU.mult).then_inc(scaled[kind], 1)

                def rhs_out(s):
                    for f in range(2):
                        ps = from_d("rhs", s, f)
                        dve.tensor_tensor(tmp[:, f, :], ps[:, 0:HH * DH], vst[:, s, f * HH * DH:(f + 1) * HH * DH], ALU.add).then_inc(tmp_ready, 1)
                        dve.wait_ge(tmp_ready, gs * 2 * (NS - 1) + 2 * (s - 1) + f + 1)
                        dve.nop().then_inc(d_read, 1)

                def add_out(kind, b, done):
                    if kind == "out":
                        dve.wait_ge(r_in[b], 16 * len(pieces(b)) * (gs + 1))
                    ps = from_d(kind, b)
                    dve.tensor_tensor(xs[:, b, :], ps[:, :], xs[:, b, :], ALU.add).then_inc(d_read, 1)
                    dve.wait_ge(d_read, after(sec, "d", (kind, b)))
                    stats(xs[:, b, :], xt6[:, b, :], xmv[:, b, :], done)

                def cross_queries(b):
                    dve.wait_ge(rstd2, gs * NB + b + 1)
                    if b >= 1:
                        dve.wait_ge(xq_rot, gs * NB + b)
                    link(dve.tensor_scalar(xa[:, 0, :], xs[:, b, :], xmv[:, b, 0:1], xrs[:, b:b + 1], ALU.subtract, ALU.mult))
                    link(dve.tensor_tensor(xa[:, 0, :], xa[:, 0, :], qnw_s[:, :], ALU.mult))
                    link(dve.tensor_tensor(halves(xa[:, 1, :]), swapped(xa[:, 0, :]), table2(b, 1, H), ALU.mult))
                    dve.tensor_tensor(heads(xa[:, 0, :]), heads(xa[:, 0, :]), table(b, 0, H), ALU.mult).then_inc(xq_prod, 1)

                def norm_ffn(b):
                    dve.wait_ge(rstd3, gs * NB + b + 1)
                    if b >= 2:
                        dve.wait_ge(a_full, after(sec, "a", ("norm3", b - 2)))
                    else:
                        dve.wait_ge(xq_rot, (gs + 1) * NB)
                    dve.tensor_scalar(xa[:, b % 2, :], xs[:, b, :], xmv[:, b, 0:1], xrs[:, b:b + 1],
                                      ALU.subtract, ALU.mult).then_inc(norm3, 1)

                def hidden_out(b):
                    ps = from_d("hid", b)
                    dve.tensor_tensor(h1[:, b, :], ps[:, 0:E * R], bd_s[:, :], ALU.add)
                    dve.tensor_tensor(lg[:, b, :], ps[:, E * R:E * R + E], brb[:, :], ALU.add).then_inc(d_read, 1)

                def gate_logits(a):
                    bs = slice(2 * a, 2 * a + 2)
                    dve.wait_ge(d_read, after(sec, "d", ("hid", 2 * a + 1)))
                    link(dve.tensor_reduce(lmax[:, bs], lg[:, bs, :], AX.X, ALU.max))
                    dve.tensor_tensor(lg[:, bs, :], lg[:, bs, :], lmax[:, bs].unsqueeze(2).broadcast_to([P, 2, E]), ALU.subtract).then_inc(gate_max, 1)

                def gating(a):
                    bs = slice(2 * a, 2 * a + 2)
                    dve.wait_ge(gate_exp, gs * 2 + a + 1)
                    mine = ex[:, bs, :].unsqueeze(3).broadcast_to([P, 2, E, E])
                    other = ex[:, bs, :].unsqueeze(2).broadcast_to([P, 2, E, E])
                    dve.tensor_tensor(cmp1[:, :, :, :], other, mine, ALU.is_gt)
                    link(dve.tensor_tensor(cmp2[:, :, :, :], other, mine, ALU.is_equal))
                    link(dve.tensor_tensor(cmp2[:, :, :, :].rearrange("p b e f -> p b (e f)"), cmp2[:, :, :, :].rearrange("p b e f -> p b (e f)"),
                                           before[:, :, :].rearrange("p e f -> p (e f)").unsqueeze(1).broadcast_to([P, 2, E * E]), ALU.mult))
                    link(dve.tensor_tensor(cmp1[:, :, :, :], cmp1[:, :, :, :], cmp2[:, :, :, :], ALU.add))
                    link(dve.tensor_reduce(rank[:, bs, :], cmp1[:, :, :, :], AX.X, ALU.add))
                    link(dve.scalar_tensor_tensor(wsel[:, bs, :], rank[:, bs, :], 2.0, ex[:, bs, :], ALU.is_lt, ALU.mult))
                    link(dve.tensor_reduce(wsum[:, bs], wsel[:, bs, :], AX.X, ALU.add))
                    link(dve.reciprocal(wsum[:, bs], wsum[:, bs]))
                    w = gates[:, 0:NB * E].rearrange("p (b e) -> p b e", b=NB)
                    link(dve.tensor_tensor(w[:, bs, :], wsel[:, bs, :], wsum[:, bs].unsqueeze(2).broadcast_to([P, 2, E]), ALU.mult))
                    for b in (2 * a, 2 * a + 1):
                        hb = h1[:, b, :].rearrange("p (e r) -> p e r", e=E)
                        dve.scalar_tensor_tensor(hb, hb, 0.0, w[:, b, :].unsqueeze(2).broadcast_to([P, E, R]),
                                                 ALU.max, ALU.mult).then_inc(hw_ready, 1)

                def ffn_out(b):
                    ps = from_d("ffn", b)
                    dve.tensor_tensor(xs[:, b, :], ps[:, :], xs[:, b, :], ALU.add).then_inc(d_read, 1)

                def invert(g):
                    y = blk[:, g, :, :]
                    dve.wait_ge(blk_in[g], 16 * (gk + 1))
                    for k in range(1, Q - 1):
                        w = Q - 1 - k
                        o = outer2[:, 0:k * w].rearrange("p (j i) -> p j i", j=k)
                        link(dve.tensor_tensor(o, y[:, 0:k, k:k + 1].broadcast_to([P, k, w]),
                                               y[:, k:k + 1, k + 1:Q].broadcast_to([P, k, w]), ALU.mult))
                        link(dve.tensor_tensor(y[:, 0:k, k + 1:Q], y[:, 0:k, k + 1:Q], o, ALU.add))
                    dve.memset(y.rearrange("p j i -> p (j i)")[:, 0:Q * Q:Q + 1], 1.0).then_inc(inv_done[g], 1)

                lo, hi = range(0, 2), range(2, NC)
                if K:
                    row_stats(0); row_stats(1); norm(0); norm(1); rope_products(0, "k")
                if S:
                    row_max("att", 1, [0]); rhs_out(1); row_max("att", 1, [1, 2]); rhs_out(2); row_max("att", 1, [3])
                if S:
                    rhs_out(3)
                if K:
                    rope_products(0, "q")
                if S:
                    scale("att", 1)
                if K:
                    beta_out(0)
                if S:
                    add_out("out", 0, stats2); row_max("att", 2); context_stats(); scale("att", 2)
                if K:
                    rope_products(1, "k")
                if S:
                    add_out("out", 1, stats2); row_max("att", 3, lo)
                if K:
                    rope_products(1, "q")
                if K:
                    row_stats(2)
                if S:
                    row_max("att", 3, hi)
                if K:
                    norm(2); beta_out(1)
                if S:
                    scale("att", 3)
                if S:
                    context_keys(); add_out("out", 2, stats2)
                if K:
                    row_max("low", 0, lo); rope_products(2, "k"); row_max("low", 0, hi); rope_products(2, "q")
                    row_stats(3); low_factors(0); beta_out(2); norm(3)
                if S:
                    add_out("out", 3, stats2)
                if K:
                    low_out(0, lo); row_max("low", 1, lo); low_out(0, hi)
                if S:
                    cross_queries(0)
                if K:
                    rope_products(3, "k"); row_max("low", 1, hi)
                if S:
                    cross_queries(1)
                if K:
                    rope_products(3, "q"); low_factors(1); scale_low(1, range(NC))
                if S:
                    row_max("x", 0, lo)
                if K:
                    beta_out(3); low_out(1, lo)
                if S:
                    row_max("x", 0, [2])
                if K:
                    low_out(1, hi)
                if S:
                    row_max("x", 0, [3]); scale("x", 0, lo)
                for b in (0, 1):
                    if K and b == 1:
                        low_out(2, lo)
                    if K:
                        row_max("low", b + 2, [0])
                    if K and b == 1:
                        low_out(2, hi)
                    if S and b == 1:
                        scale("x", b, lo)
                    if K:
                        row_max("low", b + 2, [1, 2])
                    if K:
                        row_max("low", b + 2, [3])
                    if S:
                        scale("x", b, [2]); scale("x", b, [3]); row_max("x", b + 1, [0])
                        if b == 0:
                            cross_queries(2)
                        row_max("x", b + 1, [1])
                    if K:
                        low_factors(b + 2); scale_low(b + 2, lo)
                    if S and b == 0:
                        row_max("x", 1, [2])
                    if K:
                        scale_low(b + 2, hi)
                    if K and b == 1:
                        low_out(3, lo)
                    if S and b == 1:
                        row_max("x", 2, [2])
                    if K and b == 1:
                        low_out(3, hi)
                    if S and b == 1:
                        cross_queries(3)
                    if S:
                        row_max("x", b + 1, [3])
                    if S and b == 1:
                        scale("x", 2, lo)
                    if S:
                        add_out("xout", b, stats3)
                if S:
                    scale("x", 2, [2]); scale("x", 2, [3]); row_max("x", 3, [0])
                    row_max("x", 3, [1]); norm_ffn(0); row_max("x", 3, [2]); row_max("x", 3, [3])
                    scale("x", 3, lo); add_out("xout", 2, stats3); hidden_out(0); norm_ffn(1)
                if K:
                    row_max("att", 0, lo)
                if S:
                    scale("x", 3, [2]); scale("x", 3, [3])
                if K:
                    row_max("att", 0, [2])
                if S:
                    norm_ffn(2); add_out("xout", 3, stats3); hidden_out(1); gate_logits(0); hidden_out(2)
                if K:
                    row_max("att", 0, [3])
                if S:
                    norm_ffn(3); gating(0); hidden_out(3); gate_logits(1); gating(1); ffn_out(0); ffn_out(1)
                elif K:
                    invert(1)
                if K:
                    scale("att", 0)
                if S:
                    ffn_out(2); ffn_out(3)
                if sec.name != "last":
                    assert links[0] == (FIRST if sec.name == "first" else BOTH)["dve"], links

            section(first_section())
            dve.wait_ge(loaded, 16 * N_LOADS)
            dve.tensor_scalar(brb[:, :], brb[:, :], BONUS, None, ALU.add).then_inc(table_done, 1)
            dve.wait_ge(table_done, 4)
            with dve.Fori(0, TURNS - 1) as t:
                section(both_section(t))
            section(last_section(TURNS))

        @block.gpsimd
        def _(pool):
            pool.memset(ident[:, :], 0.0).then_inc(pool_step, 1)
            pool.memset(c_mhalf[:, :], -0.5).then_inc(pool_step, 1)
            pool.memset(c_eps[:, :], EPS).then_inc(pool_step, 1)
            pool.memset(c_1eps[:, :], 1.0 + EPS).then_inc(pool_step, 1)
            pool.memset(c_eps2[:, :], EPS * EPS).then_inc(pool_step, 1)
            pool.wait_ge(pool_step, 5)
            pool.affine_select(out=ident[:, :], in_=ident[:, :], compare_op=ALU.not_equal, fill=1.0, base=0,
                               pattern=[[-1, P]], channel_multiplier=1).then_inc(pool_const, 1)

            def section(sec):
                S, K, gs, gk = sec.S, sec.K, sec.gs, sec.gk
                links = [0]

                def link(ins):
                    links[0] += 1
                    ins.then_inc(pool_link, 1)
                    pool.wait_ge(pool_link, sec.base["pool"] + links[0])

                def layer_rstd(b, m, v, r, ready, g, done):
                    pool.wait_ge(ready, g * NB + b + 1)
                    link(pool.tensor_tensor(v[:, b:b + 1], m[:, b, 1:2], c_eps[:, b:b + 1], ALU.add))
                    pool.tensor_tensor(r[:, b:b + 1], v[:, b:b + 1], c_mhalf[:, b:b + 1], ALU.pow).then_inc(done, 1)

                def rstd_rows(b):
                    layer_rstd(b, mv, va, rs, stats1, gk, rstd1)

                def rstd_ffn(b):
                    layer_rstd(b, xmv, xva, xrs, stats3, gs, rstd3)

                def rstd_context():
                    pool.wait_ge(cstats, (gs + 1) * NB)
                    link(pool.tensor_tensor(cva[:, :], cmv[:, :, 0], cmv[:, :, 0], ALU.mult))
                    link(pool.tensor_tensor(cva[:, :], cva[:, :], cmv[:, :, 1], ALU.add))
                    link(pool.tensor_tensor(cva[:, :], cva[:, :], c_eps[:, :], ALU.add))
                    pool.tensor_tensor(crs[:, :], cva[:, :], c_mhalf[:, :], ALU.pow).then_inc(crstd, 1)

                def rotate(b, name):
                    kq = 0 if name == "k" else 1
                    pool.wait_ge(d_read, after(sec, "d", (name, b)))
                    pool.tensor_tensor(tc[:, kq, :], tc[:, kq, :], ts[:, kq, :], ALU.add).then_inc(rot_done, 1)

                def scale_low(b):
                    pool.wait_ge(coef_low, gk * NB + b + 1)
                    a = half(sec, "low", b)
                    for c in range(NC):
                        sl = prob[:, a, c, :, :]
                        pool.tensor_tensor(sl, sl, coef[:, a, c * HC:(c + 1) * HC].unsqueeze(2).broadcast_to([P, HC, P]),
                                           ALU.mult).then_inc(scaled["low"], 1)

                def invert(g, k0, k1):
                    y = blk[:, g, :, :]
                    if k0 == 1:
                        pool.wait_ge(blk_in[g], 16 * (gk + 1))
                    for k in range(k0, k1):
                        w = Q - 1 - k
                        o = outer[:, 0:k * w].rearrange("p (j i) -> p j i", j=k)
                        link(pool.tensor_tensor(o, y[:, 0:k, k:k + 1].broadcast_to([P, k, w]),
                                                y[:, k:k + 1, k + 1:Q].broadcast_to([P, k, w]), ALU.mult))
                        link(pool.tensor_tensor(y[:, 0:k, k + 1:Q], y[:, 0:k, k + 1:Q], o, ALU.add))
                    if k1 == Q - 1:
                        pool.nop().then_inc(passed["pool"], 1)
                        pool.memset(y.rearrange("p j i -> p (j i)")[:, 0:Q * Q:Q + 1], 1.0).then_inc(inv_done[g], 1)

                def rstd_cross(b):
                    pool.wait_ge(stats2, gs * NB + b + 1)
                    link(pool.tensor_tensor(xva[:, b:b + 1], xmv[:, b, 1:2], c_1eps[:, b:b + 1], ALU.mult))
                    link(pool.tensor_tensor(xva[:, b:b + 1], xva[:, b:b + 1], c_eps2[:, b:b + 1], ALU.add))
                    pool.tensor_tensor(xrs[:, b:b + 1], xva[:, b:b + 1], c_mhalf[:, b:b + 1], ALU.pow).then_inc(rstd2, 1)

                def rotate_cross(b):
                    pool.wait_ge(xq_prod, gs * NB + b + 1)
                    if b == 1:
                        pool.wait_ge(a_full, after(sec, "a", ("xq", 0)))
                    elif b >= 2 and K:
                        pool.wait_ge(a_full, after(sec, "a", ("qT", 3)))
                    pool.tensor_tensor(queries[b].rearrange("p (c g d) -> p g c d", c=NC, g=G),
                                       xa[:, 0, :].rearrange("p (g c d) -> p g c d", g=G, c=NC),
                                       xa[:, 1, :].rearrange("p (g c d) -> p g c d", g=G, c=NC), ALU.add).then_inc(xq_rot, 1)

                if K:
                    rstd_rows(0); rstd_rows(1)
                if S:
                    pool.wait_ge(inv_out[0], 16 * (gs + 1))
                    pool.nop().then_inc(passed["pool"], 1)
                    pool.wait_ge(inv_out[1], 16 * (gs + 1))
                    pool.nop().then_inc(passed["pool"], 1)
                    pool.memset(us[:, :, :], 0.0).then_inc(u_zero, 1)
                if K:
                    rotate(0, "k"); rotate(0, "q")
                if S:
                    rstd_cross(0); rstd_context()
                if K:
                    rotate(1, "k")
                if S:
                    rstd_cross(1)
                if K:
                    rotate(1, "q"); rstd_rows(2)
                if S:
                    rstd_cross(2)
                if K:
                    rotate(2, "k"); rotate(2, "q"); rstd_rows(3); scale_low(0)
                if S:
                    rstd_cross(3); rotate_cross(0)
                if K:
                    rotate(3, "k"); rotate(3, "q")
                if S:
                    rotate_cross(1)
                if K:
                    invert(0, 1, 8)
                if S:
                    rotate_cross(2)
                if K:
                    invert(0, 8, 19)
                if S:
                    rstd_ffn(0)
                if K:
                    invert(0, 19, 30)
                if S:
                    rotate_cross(3)
                if K:
                    invert(0, 30, Q - 1)
                if S and K:
                    invert(1, 1, 5)
                if S:
                    rstd_ffn(1)
                if S and K:
                    invert(1, 5, 15)
                if S:
                    rstd_ffn(2)
                if S and K:
                    invert(1, 15, 20)
                if S:
                    rstd_ffn(3)
                if S and K:
                    invert(1, 20, Q - 1)
                if sec.name != "last":
                    assert links[0] == (FIRST if sec.name == "first" else BOTH)["pool"], links

            section(first_section())
            with pool.Fori(0, TURNS - 1) as t:
                section(both_section(t))
            section(last_section(TURNS))

        @block.sync
        def _(sp):
            sp.nop().then_inc(stored, 1)
            sp.dma_start(lowT[:, 0, 0:2 * NB, :],
                         mask_d.rearrange("p a b j -> p (a b) j")).then_inc(mask_in, 16)
            for b in (0, 1):
                for t0, p0, n in pieces(b):
                    sp.dma_start(xn[p0:p0 + n, b, :], x[b, t0:t0 + n, :]).then_inc(x_in[b], 16)
            for dst, src in ((wk, Wk), (wq, Wq), (wv, Wv), (wb, Wb)):
                sp.dma_start(dst[:, :, :], src.rearrange("(c p) n -> p c n", p=P)).then_inc(loaded_k, 16)
            sp.dma_start(rope[:, :, :, :], rope_d).then_inc(loaded_k, 16)
            sp.dma_start(bb_s[:, :], bb.partition_broadcast(P)).then_inc(loaded_k, 16)
            sp.dma_start(notfirst[:, :], notfirst_d).then_inc(loaded_k, 16)

            def load_rest():
                sp.dma_start(wo[:, :, :], Wo.rearrange("(c p) n -> p c n", p=P)).then_inc(loaded, 16)
                for o in range(NC):
                    for c in range(NC):
                        sp.dma_start(attT[:, o * NC + c, :].rearrange("p (g d) -> p g d", g=G),
                                     w_out[o * P:(o + 1) * P, :].rearrange("p (g c d) -> p c g d", g=G, c=NC)[:, c, :, :]).then_inc(loaded, 16)
                for c in range(NC):
                    sp.dma_start(wdr[:, c, 0:E * R].rearrange("p (e r) -> p e r", e=E),
                                 Wd[:, c * P:(c + 1) * P, :].rearrange("e p r -> p e r")).then_inc(loaded, 16)
                sp.dma_start(wdr[:, :, E * R:], Wr.rearrange("(c p) e -> p c e", p=P)).then_inc(loaded, 16)
                sp.dma_start(wu[:, :], Wu.rearrange("e r d -> (e r) d")).then_inc(loaded, 16)
                sp.wait_ge(bu_zero, 1)
                sp.dma_start(bu_s[0:E, :], bu).then_inc(loaded, 16)
                sp.dma_start(qnw_s[:, :], qnw.partition_broadcast(P)).then_inc(loaded, 16)
                sp.dma_start(knw_s[:, :], knw.partition_broadcast(P)).then_inc(loaded, 16)
                sp.dma_start(brb[:, :], br.partition_broadcast(P)).then_inc(loaded, 16)
                sp.dma_start(bd_s[:, :], bd.rearrange("e r -> (e r)").partition_broadcast(P)).then_inc(loaded, 16)
                sp.dma_start(before[:, :, :], before_d).then_inc(loaded, 16)

            def section(sec):
                S, K, gs, gk = sec.S, sec.K, sec.gs, sec.gk

                def wait(semaphore, value):
                    sp.wait_ge(semaphore, value)
                    sp.nop().then_inc(passed["sp"], 1)

                def load(dst, src, g, b, done):
                    for t0, p0, n in pieces(b):
                        sp.dma_start(dst[p0:p0 + n, :],
                                     src[bass.ds(g * NB + b, 1), t0:t0 + n, :].rearrange("o t d -> (o t) d")).then_inc(done, 16)

                def rows_in(b):
                    if b >= 2:
                        wait(a_full, after(sec, "a", ("norm", b - 2)))
                    load(xn[:, b % 2, :], x, gk, b, x_in[b])

                def spread(n, g):
                    b = n % NB
                    for r in range(HC):
                        sp.dma_start(kbd[Q * r:Q * r + Q, n % 2, :, r, :], kT[Q * r:Q * r + Q, b, :, :]).then_inc(kbd_in[n % 2], 16)

                def keys_for_keys(b):
                    if b >= 2:
                        wait(s_full, after(sec, "s", ("low", b - 2, NC - 1)))
                    elif S:
                        wait(s_full, after(sec, "s", ("att", b + 2, NC - 1)))
                    wait(a_read, after(sec, "a", ("kT", b)))
                    spread(b, gk)

                def keys_for_queries(b, g):
                    if b == 2:
                        wait(s_full, sec.base["s"])
                    elif b == 3:
                        wait(s_full, after(sec, "s", ("att", 1, NC - 1)))
                    else:
                        wait(s_full, after(sec, "s", ("low", b + 2, NC - 1)))
                    spread(NB + b, g)

                def blocks_out(b):
                    wait(d_read, after(sec, "d", ("low", b, NC - 1)))
                    for s in range(NS):
                        q = Q * ((s + b) % NS)
                        sp.dma_start(blk_d[b, :, q // Q].rearrange("h j i -> j h i"),
                                     lowT[q:q + Q, b, :, q:q + Q]).then_inc(blk_out[b], 16)

                def blocks_in(g):
                    for b in (2 * g, 2 * g + 1):
                        wait(blk_out[b], 16 * NS * (gk + 1))
                    sp.dma_start(blk[:, g, :, :].rearrange("p j i -> p (j i)"),
                                 blk_d[2 * g:2 * g + 2].rearrange("b h q j i -> (b h q) (j i)")).then_inc(blk_in[g], 16)

                def inverses_out(g):
                    wait(inv_done[g], gk + 1)
                    sp.dma_start(inv_d[2 * g:2 * g + 2].rearrange("b h q j i -> (b h q) (j i)"),
                                 blk[:, g, :, :].rearrange("p j i -> p (j i)")).then_inc(inv_out[g], 16)

                def inverses_in(g):
                    wait(inv_out[g], 16 * (gk + 1))
                    if g == 1:
                        if S:
                            wait(a_full, after(sec, "a", ("norm3", NB - 1)))
                        for b in (2, 3):
                            sp.dma_start(inv23[b - 2], inv_d[b].rearrange("h q j i -> (q j) h i")).then_inc(inv_in[g], 16)
                        return
                    for b in (0, 1):
                        for s in range(NS):
                            q = Q * ((s + b) % NS)
                            sp.dma_start(lowT[q:q + Q, b, :, q:q + Q], inv_d[b, :, q // Q].rearrange("h j i -> j h i")).then_inc(inv_in[g], 16)

                if K and not S:
                    load_rest()
                if S:
                    wait(d_full, sec.base["d"])
                    for b in range(NB):
                        load(ctx[:, b, :], ctx_512, gs, b, c_in[b])
                    wait(stored, gs * 16 * (2 * NB - 1) + 1)
                    for b in range(NB):
                        load(xs[:, b, :], x, gs, b, r_in[b])
                    keys_for_queries(2, gs); keys_for_queries(3, gs)
                if K:
                    rows_in(2); keys_for_keys(0); rows_in(3); keys_for_keys(1)
                    blocks_out(0); keys_for_keys(2)
                    blocks_out(1); blocks_in(0); keys_for_keys(3); keys_for_queries(0, gk)
                    blocks_out(2); keys_for_queries(1, gk)
                    blocks_out(3); blocks_in(1)
                    inverses_out(0); inverses_in(0); inverses_out(1); inverses_in(1)
                if S:
                    for b in range(NB):
                        wait(d_read, after(sec, "d", ("ffn", b)))
                        for t0, p0, n in pieces(b):
                            sp.dma_start(out[bass.ds(gs * NB + b, 1), t0:t0 + n, :].rearrange("o t d -> (o t) d"),
                                         xs[p0:p0 + n, b, :]).then_inc(stored, 16)

            section(first_section())
            with sp.Fori(0, TURNS - 1) as t:
                section(both_section(t))
            section(last_section(TURNS))
            sp.wait_ge(stored, TURNS * 16 * (2 * NB - 1) + 1)


_INS = ["x", "ctx_512", "L0_attn_Wq", "L0_attn_Wk", "L0_attn_Wv", "L0_attn_Wb", "L0_attn_bb", "L0_attn_Wo",
        "L0_xattn_q_norm_w", "L0_xattn_k_norm_w", "L0_xattn_w_out", "L0_ffn_Wr", "L0_ffn_br", "L0_ffn_Wd", "L0_ffn_bd",
        "L0_ffn_Wu", "L0_ffn_bu"]


def kernel(**inputs):
    import numpy as _np
    import concourse.bacc as _bacc
    from concourse import mybir as _mybir
    from concourse.bass_utils import run_bass_kernel_spmd as _run

    nc = _bacc.Bacc("TRN2", target_bir_lowering=False, num_devices=1)
    arrays, args = {}, []
    for name in _INS:
        a = _np.ascontiguousarray(inputs[name])
        arrays[f"in_{name}_dram"] = a
        args.append(nc.dram_tensor(f"in_{name}_dram", a.shape, _mybir.dt.from_np(a.dtype), kind="ExternalInput").ap())
    args.append(nc.dram_tensor("out_0_dram", inputs["x"].shape, _mybir.dt.float32, kind="ExternalOutput").ap())
    decoder_layer(nc, *args)
    r = _run(nc, [arrays], core_ids=[0])
    return r.results[0]["out_0_dram"]
```
